# Optimizing a Trainium2 kernel written in Bass

```python
import numpy as np
import jax
import jax.numpy as jnp

def _softmax(x, axis=-1):
    return jax.nn.softmax(x, axis=axis)

def _gelu(x):
    return jax.nn.gelu(x, approximate=True)

def _silu(x):
    return jax.nn.silu(x)

def _sigmoid(x):
    return jax.nn.sigmoid(x)

def _layernorm(x, axis=-1, eps=1e-05):
    m = jnp.mean(x, axis=axis, keepdims=True)
    v = jnp.var(x, axis=axis, keepdims=True)
    return (x - m) / jnp.sqrt(v + eps)

def _scatter_add(tgt, idx, src, axis=0):
    return tgt.at[idx].add(src)

def _segment_sum(src, seg, n):
    return jax.ops.segment_sum(src, seg, n)
kernel_name = 'mk_macaron_d1_jaxref_r8_41a1f5'

def setup_inputs(seed: int=0):
    np.random.seed(seed)
    _w = jnp.asarray

    def _L0_attn_setup():
        import jax, jax.numpy as jnp
        import numpy as np
        B, S, HID = (2, 256, 256)
        H, D = (16, 128)
        K = 4
        EPS_L2 = 1e-06
        EPS_RMS = 1e-05

        def _l2norm(x, eps=EPS_L2):
            return x * jax.lax.rsqrt(jnp.sum(x * x, axis=-1, keepdims=True) + eps)

        def _causal_dwconv_silu(x, w):
            y = jax.lax.conv_general_dilated(x, w, window_strides=(1,), padding=[(w.shape[0] - 1, 0)], dimension_numbers=('NWC', 'WIO', 'NWC'), feature_group_count=x.shape[-1])
            return jax.nn.silu(y)

        def _delta_rule(q, k, v, g, beta, scale):
            qs = (q * scale).transpose(1, 0, 2, 3)
            ks = k.transpose(1, 0, 2, 3)
            vs = v.transpose(1, 0, 2, 3)
            gs = g.transpose(1, 0, 2, 3)
            bs = beta.transpose(1, 0, 2)

            def step(Sst, inp):
                qt, kt, vt, gt, bt = inp
                Sst = Sst * jnp.exp(gt)[..., :, None]
                err = vt - jnp.einsum('bhk,bhkv->bhv', kt, Sst)
                Sst = Sst + bt[..., None, None] * kt[..., :, None] * err[..., None, :]
                ot = jnp.einsum('bhk,bhkv->bhv', qt, Sst)
                return (Sst, ot)
            S0 = jnp.zeros((q.shape[0], q.shape[2], q.shape[3], v.shape[3]), q.dtype)
            _, outs = jax.lax.scan(step, S0, (qs, ks, vs, gs, bs))
            return outs.transpose(1, 0, 2, 3)
        key = jax.random.key(seed)
        ks = jax.random.split(key, 20)
        sh = 1.0 / np.sqrt(HID)
        sd = 1.0 / np.sqrt(D)
        inp = {'hidden_states': jax.random.normal(ks[0], (B, S, HID), jnp.float32), 'Wq': jax.random.normal(ks[1], (HID, H * D), jnp.float32) * sh, 'Wk': jax.random.normal(ks[2], (HID, H * D), jnp.float32) * sh, 'Wv': jax.random.normal(ks[3], (HID, H * D), jnp.float32) * sh, 'conv_q': jax.random.normal(ks[4], (K, 1, H * D), jnp.float32) * 0.5, 'conv_k': jax.random.normal(ks[5], (K, 1, H * D), jnp.float32) * 0.5, 'conv_v': jax.random.normal(ks[6], (K, 1, H * D), jnp.float32) * 0.5, 'Wb': jax.random.normal(ks[7], (HID, H), jnp.float32) * sh, 'Wfa': jax.random.normal(ks[8], (HID, D), jnp.float32) * sh, 'Wfb': jax.random.normal(ks[9], (D, H * D), jnp.float32) * sd, 'Wga': jax.random.normal(ks[10], (HID, D), jnp.float32) * sh, 'Wgb': jax.random.normal(ks[11], (D, H * D), jnp.float32) * sd, 'A_log': jnp.log(jax.random.uniform(ks[12], (1, 1, H, 1), jnp.float32, 1e-09, 16.0)), 'dt_bias': jnp.ones((H * D,), jnp.float32), 'rms_scale': jnp.ones((D,), jnp.float32), 'Wo': jax.random.normal(ks[13], (H * D, HID), jnp.float32) * sd}
        return inp
    _L0_attn_in = _L0_attn_setup()

    def _L0_ffn_setup():
        import jax, jax.numpy as jnp
        import numpy as np
        B, S, D, E, R, TOP_K = (4, 512, 256, 6, 16, 2)
        key = jax.random.key(seed)
        ks = jax.random.split(key, 9)
        scale = 0.02
        return {'x': jax.random.normal(ks[0], (B, S, D), dtype=jnp.float32), 'W_base': jax.random.normal(ks[1], (D, D), dtype=jnp.float32) * scale, 'b_base': jax.random.normal(ks[2], (D,), dtype=jnp.float32) * scale, 'A_s': jax.random.normal(ks[3], (D, R), dtype=jnp.float32) * scale, 'B_s': jax.random.normal(ks[4], (R, D), dtype=jnp.float32) * scale, 'A_r': jax.random.normal(ks[5], (E, D, R), dtype=jnp.float32) * scale, 'B_r': jax.random.normal(ks[6], (E, R, D), dtype=jnp.float32) * scale, 'W_router': jax.random.normal(ks[7], (D, E), dtype=jnp.float32) * scale, 'b_router': jax.random.normal(ks[8], (E,), dtype=jnp.float32) * scale}
    _L0_ffn_in = _L0_ffn_setup()
    _d = {'L0_attn_hidden_states': _L0_attn_in['hidden_states'], 'L0_attn_Wq': _L0_attn_in['Wq'], 'L0_attn_Wk': _L0_attn_in['Wk'], 'L0_attn_Wv': _L0_attn_in['Wv'], 'L0_attn_conv_q': _L0_attn_in['conv_q'], 'L0_attn_conv_k': _L0_attn_in['conv_k'], 'L0_attn_conv_v': _L0_attn_in['conv_v'], 'L0_attn_Wb': _L0_attn_in['Wb'], 'L0_attn_Wfa': _L0_attn_in['Wfa'], 'L0_attn_Wfb': _L0_attn_in['Wfb'], 'L0_attn_Wga': _L0_attn_in['Wga'], 'L0_attn_Wgb': _L0_attn_in['Wgb'], 'L0_attn_A_log': _L0_attn_in['A_log'], 'L0_attn_dt_bias': _L0_attn_in['dt_bias'], 'L0_attn_rms_scale': _L0_attn_in['rms_scale'], 'L0_attn_Wo': _L0_attn_in['Wo'], 'L0_ffn_W_base': _L0_ffn_in['W_base'], 'L0_ffn_b_base': _L0_ffn_in['b_base'], 'L0_ffn_A_s': _L0_ffn_in['A_s'], 'L0_ffn_B_s': _L0_ffn_in['B_s'], 'L0_ffn_A_r': _L0_ffn_in['A_r'], 'L0_ffn_B_r': _L0_ffn_in['B_r'], 'L0_ffn_W_router': _L0_ffn_in['W_router'], 'L0_ffn_b_router': _L0_ffn_in['b_router']}
    _x0 = _d['L0_attn_hidden_states']
    _d['L0_attn_hidden_states'] = jax.random.normal(jax.random.fold_in(jax.random.key(seed), 1), (2, 512, 256), dtype=_x0.dtype)
    del _x0
    return _d

def reference(L0_attn_hidden_states, L0_attn_Wq, L0_attn_Wk, L0_attn_Wv, L0_attn_conv_q, L0_attn_conv_k, L0_attn_conv_v, L0_attn_Wb, L0_attn_Wfa, L0_attn_Wfb, L0_attn_Wga, L0_attn_Wgb, L0_attn_A_log, L0_attn_dt_bias, L0_attn_rms_scale, L0_attn_Wo, L0_ffn_W_base, L0_ffn_b_base, L0_ffn_A_s, L0_ffn_B_s, L0_ffn_A_r, L0_ffn_B_r, L0_ffn_W_router, L0_ffn_b_router):

    def _L0_attn_ref(hidden_states, Wq, Wk, Wv, conv_q, conv_k, conv_v, Wb, Wfa, Wfb, Wga, Wgb, A_log, dt_bias, rms_scale, Wo):
        import jax, jax.numpy as jnp
        import numpy as np
        B, S, HID = (2, 256, 256)
        H, D = (16, 128)
        K = 4
        EPS_L2 = 1e-06
        EPS_RMS = 1e-05

        def _l2norm(x, eps=EPS_L2):
            return x * jax.lax.rsqrt(jnp.sum(x * x, axis=-1, keepdims=True) + eps)

        def _causal_dwconv_silu(x, w):
            y = jax.lax.conv_general_dilated(x, w, window_strides=(1,), padding=[(w.shape[0] - 1, 0)], dimension_numbers=('NWC', 'WIO', 'NWC'), feature_group_count=x.shape[-1])
            return jax.nn.silu(y)

        def _delta_rule(q, k, v, g, beta, scale):
            qs = (q * scale).transpose(1, 0, 2, 3)
            ks = k.transpose(1, 0, 2, 3)
            vs = v.transpose(1, 0, 2, 3)
            gs = g.transpose(1, 0, 2, 3)
            bs = beta.transpose(1, 0, 2)

            def step(Sst, inp):
                qt, kt, vt, gt, bt = inp
                Sst = Sst * jnp.exp(gt)[..., :, None]
                err = vt - jnp.einsum('bhk,bhkv->bhv', kt, Sst)
                Sst = Sst + bt[..., None, None] * kt[..., :, None] * err[..., None, :]
                ot = jnp.einsum('bhk,bhkv->bhv', qt, Sst)
                return (Sst, ot)
            S0 = jnp.zeros((q.shape[0], q.shape[2], q.shape[3], v.shape[3]), q.dtype)
            _, outs = jax.lax.scan(step, S0, (qs, ks, vs, gs, bs))
            return outs.transpose(1, 0, 2, 3)
        b, s, _ = hidden_states.shape
        q = _l2norm(jnp.einsum('bsd,de->bse', hidden_states, Wq).reshape(b, s, H, D))
        k = _l2norm(jnp.einsum('bsd,de->bse', hidden_states, Wk).reshape(b, s, H, D))
        v = jnp.einsum('bsd,de->bse', hidden_states, Wv).reshape(b, s, H, D)
        q = _causal_dwconv_silu(q.reshape(b, s, -1), conv_q).reshape(b, s, H, D)
        k = _causal_dwconv_silu(k.reshape(b, s, -1), conv_k).reshape(b, s, H, D)
        v = _causal_dwconv_silu(v.reshape(b, s, -1), conv_v).reshape(b, s, H, D)
        beta = jax.nn.sigmoid(jnp.einsum('bsd,dh->bsh', hidden_states, Wb))
        g_lin = jnp.einsum('bse,ef->bsf', jnp.einsum('bsd,de->bse', hidden_states, Wfa), Wfb)
        sp = jax.nn.softplus(g_lin + dt_bias).reshape(b, s, H, D)
        g_forget = -jnp.exp(A_log) * sp
        attn = _delta_rule(q, k, v, g_forget, beta, scale=D ** (-0.5))
        gate = jnp.einsum('bse,ef->bsf', jnp.einsum('bsd,de->bse', hidden_states, Wga), Wgb).reshape(b, s, H, D)
        normed = attn * jax.lax.rsqrt(jnp.mean(attn * attn, axis=-1, keepdims=True) + EPS_RMS) * rms_scale
        out = (normed * jax.nn.sigmoid(gate)).reshape(b, s, -1)
        return jnp.einsum('bse,ed->bsd', out, Wo)

    def _L0_ffn_ref(x, W_base, b_base, A_s, B_s, A_r, B_r, W_router, b_router):
        import jax, jax.numpy as jnp
        import numpy as np
        B, S, D, E, R, TOP_K = (4, 512, 256, 6, 16, 2)
        base_out = jax.lax.stop_gradient(jnp.einsum('bsd,df->bsf', x, W_base) + b_base)
        shared_out = jnp.einsum('bsr,rf->bsf', jnp.einsum('bsd,dr->bsr', x, A_s), B_s)
        gates = jax.nn.softmax(jnp.einsum('bsd,de->bse', x, W_router) + b_router, axis=-1)
        topk_w, topk_i = jax.lax.top_k(gates, TOP_K)
        w_per_e = jnp.sum(topk_w[..., None] * jax.nn.one_hot(topk_i, E, dtype=x.dtype), axis=2)
        h = jnp.einsum('bsd,edr->bser', x, A_r)
        hw = h * w_per_e[..., None]
        routed_out = jnp.einsum('bser,erf->bsf', hw, B_r)
        return base_out + shared_out + routed_out
    x = L0_attn_hidden_states
    x = x + 0.5 * _L0_ffn_ref(_layernorm(x, axis=-1), L0_ffn_W_base, L0_ffn_b_base, L0_ffn_A_s, L0_ffn_B_s, L0_ffn_A_r, L0_ffn_B_r, L0_ffn_W_router, L0_ffn_b_router)
    x = x + _L0_attn_ref(_layernorm(x, axis=-1), L0_attn_Wq, L0_attn_Wk, L0_attn_Wv, L0_attn_conv_q, L0_attn_conv_k, L0_attn_conv_v, L0_attn_Wb, L0_attn_Wfa, L0_attn_Wfb, L0_attn_Wga, L0_attn_Wgb, L0_attn_A_log, L0_attn_dt_bias, L0_attn_rms_scale, L0_attn_Wo)
    x = x + 0.5 * _L0_ffn_ref(_layernorm(x, axis=-1), L0_ffn_W_base, L0_ffn_b_base, L0_ffn_A_s, L0_ffn_B_s, L0_ffn_A_r, L0_ffn_B_r, L0_ffn_W_router, L0_ffn_b_router)
    return x

_drawn_inputs = setup_inputs


def setup_inputs(seed=0):
    import zlib

    import numpy as np

    out = dict(_drawn_inputs(seed))
    spreads = {'L0_attn_dt_bias': (1.0, 0.6), 'L0_attn_rms_scale': (1.0, 0.2)}
    factors = {'L0_ffn_b_base': 2.902,
     'L0_ffn_A_r': 7.835,
     'L0_ffn_B_r': 7.854,
     'L0_ffn_W_router': 8.0,
     'L0_ffn_b_router': 8.0,
     'L0_ffn_A_s': 2.68,
     'L0_ffn_B_s': 2.729}
    for name, (base, spread) in spreads.items():
        noise = np.random.default_rng([zlib.crc32(name.encode()), seed]).standard_normal(out[name].shape)
        drawn = base * np.exp(spread * noise) if base else spread * noise
        out[name] = jnp.asarray(drawn.astype(out[name].dtype))
    for name, factor in factors.items():
        out[name] = (out[name] * factor).astype(out[name].dtype)
    return out
```

```python
from contextlib import ExitStack

import numpy as np
import concourse.bass as bass
from concourse import mybir

ALU = mybir.AluOpType
ACT = mybir.ActivationFunctionType
F32 = mybir.dt.float32
U8 = mybir.dt.uint8
AX = mybir.AxisListType
ds = bass.ds

P = 128
B, S, HID = 2, 512, 256
H, D = 16, 128
TAPS = 4
E, R, TOP = 6, 16, 2
T = B * S
C = 64
NCH = S // C
KT = HID // P
G = 4
NG = H // G
UN = G * P
HU = UN // 2
LEVELS = [1 << l for l in range(C.bit_length() - 1)]
NL = len(LEVELS)
EPS_L2, EPS_RMS, EPS_LN = 1e-6, 1e-5, 1e-5
SCALE = float(D) ** -0.5
SOFT_MAX = 40.0
RW = (1 + E) * R
NROW = RW + 1
DT = 3 * TAPS
ITEMS = G * B
HALF = NCH // 2


def build(nc, a, out):
    ctx = ExitStack()
    with ctx:
        def sb(name, shape):
            return ctx.enter_context(nc.sbuf_tensor(name, shape, F32))

        def sems(names):
            return [ctx.enter_context(nc.semaphore(x)) for x in names.split()]

        bank = [ctx.enter_context(nc.psum_tensor(f"bank{i}", [P, 512], F32)) for i in range(8)]

        ident = sb("ident", [P, P])
        ident4 = ident[:, :].rearrange("p (o i) -> p o i", o=1).broadcast_to((P, G, P))
        ones = sb("ones", [P, P])
        masks = ctx.enter_context(nc.sbuf_tensor("masks", [P, NL, HU], U8))
        eps = sb("eps", [P, 4])
        region = sb("region", [P, 10 * UN])

        def part(k, n=1):
            return region[:, k * UN:(k + n) * UN]

        rows1 = part(0)[:, 0:P]
        rows2 = part(0)[:, P:2 * P]
        junk = part(1, 4).rearrange("p (c d) -> p c d", c=NCH)
        sq = part(0, 2).rearrange("p (a s) -> p a s", a=2)
        rr = part(2, 2).rearrange("p (a s) -> p a s", a=2)
        zc = part(4)
        sp = part(5)
        PADW = TAPS - 1 + S
        pad = region[:, 6 * UN:6 * UN + 3 * PADW].rearrange("p (a s) -> p a s", a=3)
        rs, us, osq, og = (part(k) for k in range(4))
        oT = osq
        sdec = part(4, 2).rearrange("p (b s) -> p b s", b=B)
        kst = part(6)
        vb = part(7)
        tmat = part(8)
        es = part(9)
        chan = sb("chan", [P, DT + 1, H])
        rmsc = sb("rmsc", [P, 1])
        negA = sb("negA", [P, H])
        gchan = sb("gchan", [P, DT + 1, G])
        gnegA = sb("gnegA", [P, G])
        w_a = sb("w_a", [P, KT, RW + E])
        w_b = sb("w_b", [NROW, HID])
        w_base = sb("w_base", [P, KT, HID])
        brow = sb("brow", [1, E])
        x = sb("x", [P, NCH, HID])
        gate = sb("gate", [P, NCH, G * D])
        flat_gate = gate[:, :, :].rearrange("p c d -> p (c d)")
        hn = flat_gate[:, 0:NCH * HID].rearrange("p (c d) -> p c d", c=NCH)
        hw = flat_gate[:, NCH * HID:NCH * (HID + NROW)].rearrange("p (c r) -> p c r", c=NCH)
        hwT = flat_gate[0:NROW, NCH * (HID + NROW):NCH * (HID + NROW + P)].rearrange("p (c r) -> p c r", c=NCH)
        hT = sb("hT", [P, KT, T])
        st = sb("st", [P, 5, NCH])
        lg = sb("lg", [P, NCH, E])
        gt = sb("gt", [P, NCH, E])
        rk = sb("rk", [P, NCH, E])
        beats = sb("beats", [P, NCH, E])
        sm = sb("sm", [P, 3, NCH])
        faT = sb("faT", [P, T])
        gaT = sb("gaT", [P, NCH, B, C])
        beta16 = sb("beta16", [H, T])
        btok = sb("btok", [P, NCH, H])
        gw = sb("gw", [P, 3, KT, G * D])
        gfb = sb("gfb", [P, G * D])
        ggb = sb("ggb", [P, G * D])
        gwo = sb("gwo", [P, G, HID])
        gsel = sb("gsel", [H, G])
        qkv = sb("qkv", [P, 3, G, B, S])
        flat_q = qkv[:, 0].rearrange("p g b s -> p (g b s)")
        wfa, wga = (flat_q[:, i * KT * D:(i + 1) * KT * D].rearrange("p (k r) -> p k r", k=KT) for i in range(2))
        wbeta = flat_q[:, 2 * KT * D:2 * KT * D + KT * H].rearrange("p (k r) -> p k r", k=KT)
        fmasks = qkv[:, 1].rearrange("p g b s -> p (g b s)")[:, 0:NL * HU].rearrange("p (l n) -> p l n", l=NL)
        dec = sb("dec", [P, G, B, S])
        kq = sb("kq", [P, 2, 2, UN])
        ks = sb("ks", [P, 2, UN])
        vs = sb("vs", [P, UN])
        tots = [es] + [sb(f"tot{h}", [P, UN // h])[:, :] for h in LEVELS[1:]]
        gamma = sb("gamma", [P, 2, UN // C])
        nmat = sb("nmat", [P, NL, UN])
        fmat = sb("fmat", [P, NL - 1, UN])
        tt = sb("tt", [P, 2, UN])
        aq = sb("aq", [P, 2, UN])
        state = sb("state", [P, B, UN])
        ssq = sb("ssq", [P, 3, G])

        in_x, in_small, in_ffn, in_low, in_group, in_wo, stored = sems("in_x in_small in_ffn in_low in_group in_wo stored")
        const_ready, pool_chain, dve_chain, act_chain = sems("const_ready pool_chain dve_chain act_chain")
        rows_done, chan_ready, nega_ready = sems("rows_done chan_ready nega_ready")
        ln_centred, ln_rstd, ln_ready, ln_tr, hT_act, hT_dve = sems("ln_centred ln_rstd ln_ready ln_tr hT_act hT_dve")
        f_low, f_sub, f_exp, f_hw, f_hwT, f_hwTs, f_out, x_ready = sems("f_low f_sub f_exp f_hw f_hwT f_hwTs f_out x_ready")
        low_done, low_copied, beta_done, beta_exp, beta_ready = sems("low_done low_copied beta_done beta_exp beta_ready")
        pe_free, dve_free, act_free, pool_free = sems("pe_free dve_free act_free pool_free")
        gprep, wos_ready, state_zero = sems("gprep wos_ready state_zero")
        q_done, k_done, v_done, f_done, b_done, n_done = sems("q_done k_done v_done f_done b_done n_done")
        sq_ready, v_copied, b_copied, z_ready, z_exp, z_ln, sp_ready, dec_ready = sems(
            "sq_ready v_copied b_copied z_ready z_exp z_ln sp_ready dec_ready")
        n_ln, r_ready, normed, conv_chain, conved, silued, gate_done, gated = sems(
            "n_ln r_ready normed conv_chain conved silued gate_done gated")
        kb_ready, es_ready, ks_ready, vs_ready, kq_ready = sems("kb_ready es_ready ks_ready vs_ready kq_ready")
        diag_done, diag_ready, level_done, updated, n_ready, aq_ready = sems(
            "diag_done diag_ready level_done updated n_ready aq_ready")
        y_done, f_ready, t_done, t_ready, tt0_ready = sems("y_done f_ready t_done t_ready tt0_ready")
        vt_done, vb_ready, kst_done, kst_ready = sems("vt_done vb_ready kst_done kst_ready")
        r_done, rs_ready, u_done, us_ready, o_done = sems("r_done rs_ready u_done us_ready o_done")
        sdec_ready, s_done, state_ready = sems("sdec_ready s_done state_ready")
        osq_ready, ssq_ready, ssq_ln, rms_ready, og_ready, on_ready = sems(
            "osq_ready ssq_ready ssq_ln rms_ready og_ready on_ready")
        ot_done, ot_ready, wo_done, x_added = sems("ot_done ot_ready wo_done x_added")

        block = ctx.enter_context(nc.Block())

        def by_batch(ap):
            return [ap[b].rearrange("(c i) d -> i c d", i=C) for b in range(B)]

        def chunk(buf, c):
            return buf[:, :, :, ds(c * C, C)]

        def gbi(ap):
            return ap.rearrange("p (g b i) -> p g b i", g=G, b=B)

        def gd(ap):
            return ap.rearrange("p (g d) -> p g d", g=G)

        def half(ap, h, upper):
            if len(ap.shape) == 3:
                return ap.rearrange("p a (n t) -> p a n t", t=2 * h)[:, :, :, upper * h:upper * h + h]
            return ap.rearrange("p (n t) -> p n t", t=2 * h)[:, :, upper * h:upper * h + h]

        def blocks(ap, h):
            return ap.rearrange("p (n t) -> p n t", t=h)

        def unit(ap, u):
            return ap[:, u * P:(u + 1) * P]

        def spread(ap, n):
            return ap.rearrange("p (m o) -> p m o", o=1).broadcast_to((ap.shape[0], ap.shape[1], n))

        N_FFN = 8 + KT - 1
        N_SMALL = 6
        N_LOW = 3
        N_GROUP = 5

        @block.sync
        def _(eng):
            for b in range(B):
                eng.dma_start(x[b * C:(b + 1) * C, :, :], by_batch(a["x"])[b]).then_inc(in_x, 16)
            for dst, src in (
                    (w_a[:, :, 0:R], a["A_s"].rearrange("(k p) r -> p k r", p=P)),
                    *((w_a[:, k, R:RW].rearrange("p (e r) -> p e r", e=E),
                       a["A_r"][:, k * P:(k + 1) * P, :].rearrange("e p r -> p e r")) for k in range(KT)),
                    (w_a[:, :, RW:RW + E], a["W_router"].rearrange("(k p) r -> p k r", p=P)),
                    (brow[:, :], a["b_router"].rearrange("(a e) -> a e", a=1)),
                    (w_b[0:R, :], a["B_s"]),
                    (w_b[R:RW, :], a["B_r"].rearrange("e r d -> (e r) d")),
                    (w_b[RW:NROW, :], a["b_base"].rearrange("(a e) -> a e", a=1)),
                    (w_base[:, :, :], a["W_base"].rearrange("(k p) r -> p k r", p=P))):
                eng.dma_start(dst, src).then_inc(in_ffn, 16)
            TH = TAPS * H
            for dst, src in (
                    (rows1[0:TH, :], a["conv_q"].rearrange("t o (h d) -> (t o h) d", d=D)),
                    (rows1[TH:2 * TH, :], a["conv_k"].rearrange("t o (h d) -> (t o h) d", d=D)),
                    (rows2[0:TH, :], a["conv_v"].rearrange("t o (h d) -> (t o h) d", d=D)),
                    (rows2[TH:TH + H, :], a["dt_bias"].rearrange("(h d) -> h d", d=D)),
                    (rows2[TH + H:TH + H + 1, :], a["rms_scale"].rearrange("(a d) -> a d", a=1)),
                    (negA[:, :], a["A_log"].rearrange("a b h c -> (a b c) h").broadcast_to((P, H)))):
                eng.dma_start(dst, src).then_inc(in_small, 16)
            for dst, src in ((wfa, a["Wfa"]), (wga, a["Wga"]), (wbeta, a["Wb"])):
                eng.dma_start(dst, src.rearrange("(k p) r -> p k r", p=P)).then_inc(in_low, 16)

            def group_weights(g):
                cols = ds(g * (G * D), G * D)
                for i, w in enumerate(("Wq", "Wk", "Wv")):
                    eng.dma_start(gw[:, i], a[w].rearrange("(k p) r -> p k r", p=P)[:, :, cols]).then_inc(in_group, 16)
                eng.dma_start(gfb[:, :], a["Wfb"][:, cols]).then_inc(in_group, 16)
                eng.dma_start(ggb[:, :], a["Wgb"][:, cols]).then_inc(in_group, 16)

            def output_weights(g):
                eng.dma_start(gwo[:, :, :],
                              a["Wo"].rearrange("(h p) n -> p h n", p=P)[:, ds(g * G, G), :]).then_inc(in_wo, 16)

            group_weights(0)
            output_weights(0)
            with eng.Fori(1, NG) as g:
                eng.wait_ge(gate_done, NCH * g)
                group_weights(g)
                eng.wait_ge(pe_free, g + 1)
                output_weights(g)
            eng.wait_ge(x_ready, 2)
            for b in range(B):
                eng.dma_start(by_batch(out)[b], x[b * C:(b + 1) * C, :, :]).then_inc(stored, 16)
            eng.wait_ge(stored, 16 * B)

        def move_hT(f, kt, i):
            src = bank[2 * kt + i]
            if f == 1:
                return (hT[:, kt].rearrange("p (b c i) -> p c b i", b=B, c=NCH)[:, i * HALF:(i + 1) * HALF],
                        src[:, :].rearrange("p (c b i) -> p c b i", b=B, c=HALF))
            return hT[:, kt, i * 512:(i + 1) * 512], src[:, :]

        def run_slots(eng, slot, g):
            n0 = g * NCH
            slot(g, n0, 0, 0, scan=False)
            with eng.Fori(0, NCH // 2 - 1) as w:
                slot(g, n0 + 2 * w + 1, 2 * w + 1, 1)
                slot(g, n0 + 2 * w + 2, 2 * w + 2, 0)
            slot(g, n0 + NCH - 1, NCH - 1, 1, prepare=False)
            slot(g, n0 + NCH, NCH, 0, step=False)

        def barrier(eng, own, g):
            for s in (pe_free, dve_free, act_free, pool_free):
                if s is not own:
                    eng.wait_ge(s, g + 1)

        @block.gpsimd
        def _(eng):
            eng.memset(ident[:, :], 0.0)
            eng.memset(ones[:, :], 1.0)
            eng.memset(fmasks, 1.0)
            for i, v in enumerate((EPS_L2, EPS_RMS, EPS_LN, float(np.log(SCALE)))):
                eng.memset(eps[:, i:i + 1], v)
            eng.memset(nmat[:, :, :], 0.0).then_inc(pool_chain, 1)
            eng.wait_ge(pool_chain, 1)
            eng.affine_select(out=ident[:, :], in_=ident[:, :], compare_op=ALU.not_equal, fill=1.0,
                              base=0, pattern=[[-1, P]], channel_multiplier=1)

            def level_mask(l, base, step, mult):
                h = LEVELS[l]
                v = fmasks[:, l, :].rearrange("p (u n t) -> p u n t", u=G, t=h)
                return eng.affine_select(out=v, in_=v, compare_op=ALU.is_ge, fill=0.0, base=base,
                                         pattern=[[0, G], [step, P // (2 * h)], [0, h]], channel_multiplier=mult)

            for l, h in enumerate(LEVELS):
                last = level_mask(l, 0, -2 * h, 1)
            last.then_inc(pool_chain, 1)
            eng.wait_ge(pool_chain, 2)
            for l, h in enumerate(LEVELS):
                level_mask(l, h - 1, 2 * h, -1)
            for l in range(1, NL):
                last = eng.tensor_copy(gd(fmat[:, l - 1]), ident4)
            last.then_inc(pool_chain, 1)
            eng.wait_ge(pool_chain, 3)
            eng.tensor_copy(masks[:, :, :], fmasks).then_inc(const_ready, 1)
            eng.drain().then_inc(pool_free, 1)

            def slot(g, n, c, p, step=True, scan=True, prepare=True):
                m, q = n - 1, 1 - p
                if scan:
                    eng.wait_ge(state_ready, B * m + g + 1)
                    eng.wait_ge(updated, NL * n)
                    for b in range(B):
                        decay = gamma[:, q].rearrange("p (g b) -> p b g", b=B)[:, b, :]
                        last = eng.tensor_tensor(gd(sdec[:, b]), gd(state[:, b]), spread(decay, D), ALU.mult)
                    last.then_inc(sdec_ready, 1)
                if step:
                    eng.wait_ge(n_ready, NL * n + 1)
                    eng.tensor_tensor(gd(tt[:, p]), ident4, gd(nmat[:, 0]), ALU.subtract).then_inc(tt0_ready, 1)
                if scan:
                    eng.wait_ge(rms_ready, n)
                    eng.wait_ge(og_ready, n)
                    eng.tensor_tensor(gd(og), gd(og), spread(ssq[:, 2, :], D), ALU.mult).then_inc(on_ready, 1)
            with eng.Fori(0, NG) as g:
                n0 = g * NCH
                barrier(eng, pool_free, g)
                eng.wait_ge(silued, 3 * g + 3)
                run_slots(eng, slot, g)
                eng.drain().then_inc(pool_free, 1)

        @block.scalar
        def _(eng):
            chain = [0]

            def link(ins):
                chain[0] += 1
                ins.then_inc(act_chain, 1)
                eng.wait_ge(act_chain, chain[0])

            def layer_norm(f):
                eng.wait_ge(ln_centred, f + 1)
                for c in range(NCH):
                    last = eng.activation(junk[:, c], hn[:, c], ACT.Square, accum_out=st[:, 2, c:c + 1])
                link(last)
                link(eng.activation(st[:, 3], st[:, 2], ACT.Ln, bias=eps[:, 2:3], scale=1.0 / HID))
                eng.activation(st[:, 4], st[:, 3], ACT.Exp, scale=-0.5).then_inc(ln_rstd, 1)
                for i in range(2):
                    eng.wait_ge(ln_tr, 4 * f + i + 1)
                    eng.activation(*move_hT(f, 0, i), ACT.Copy).then_inc(hT_act, 1)

            def feed_forward(j):
                eng.wait_ge(f_sub, j + 1)
                eng.activation(gt[:, :, :], lg[:, :, :], ACT.Exp).then_inc(f_exp, 1)
                for i in range(2):
                    eng.wait_ge(f_hwT, 2 * j + i + 1)
                    eng.activation(hwT[:, i * HALF:(i + 1) * HALF, :].rearrange("p c t -> p (c t)"),
                                   bank[6 + i][0:NROW, :], ACT.Copy).then_inc(f_hwTs, 1)

            eng.wait_ge(const_ready, 1)
            eng.wait_ge(in_small, 16 * N_SMALL)
            link(eng.activation(negA[:, :], negA[:, :], ACT.Exp))
            eng.activation(negA[:, :], negA[:, :], ACT.Copy, scale=-1.0).then_inc(nega_ready, 1)
            layer_norm(0)
            feed_forward(0)
            layer_norm(1)
            for b in range(B):
                eng.wait_ge(low_done, b + 1)
                eng.activation(faT[:, b * S:(b + 1) * S], bank[4 + b][:, :], ACT.Copy).then_inc(low_copied, 1)
            for b in range(B):
                eng.wait_ge(low_done, B + b + 1)
                eng.activation(gaT[:, :, b, :], bank[6 + b][:, :].rearrange("p (c i) -> p c i", i=C),
                               ACT.Copy).then_inc(low_copied, 1)
            eng.wait_ge(beta_done, 1)
            for b in range(B):
                eng.activation(beta16[:, b * S:(b + 1) * S], bank[b][0:H, :], ACT.Exp, scale=-1.0)
            eng.activation(btok[:, :, :].rearrange("p c h -> p (c h)"), bank[2][:, 0:NCH * H], ACT.Exp,
                           scale=-1.0).then_inc(beta_exp, 1)
            eng.drain().then_inc(act_free, 1)

            def item(g, hh, b):
                j = hh * B + b
                i = g * ITEMS + j
                eng.wait_ge(q_done, i + 1)
                if j:
                    eng.wait_ge(n_done, 2 * i)
                eng.activation(sq[:, 0], bank[0][:, :], ACT.Square).then_inc(sq_ready, 1)
                eng.wait_ge(k_done, i + 1)
                eng.activation(sq[:, 1], bank[1][:, :], ACT.Square).then_inc(sq_ready, 1)
                eng.wait_ge(z_ready, i + 1)
                eng.activation(zc, zc, ACT.Exp).then_inc(z_exp, 1)
                eng.wait_ge(v_done, i + 1)
                if j:
                    eng.wait_ge(conved, 3 * i - 2)
                eng.activation(pad[:, 2, TAPS - 1:], bank[2][:, :], ACT.Copy).then_inc(v_copied, 1)
                eng.wait_ge(z_exp, i + 1)
                if j:
                    eng.wait_ge(dec_ready, i)
                eng.activation(sp, zc, ACT.Ln, bias=1.0).then_inc(z_ln, 1)
                for t in range(2):
                    eng.wait_ge(n_done, 2 * i + t + 1)
                    if j:
                        eng.wait_ge(normed, 2 * i - 1 + t)
                    eng.activation(rr[:, t], bank[5 + t][:, :], ACT.Ln, bias=eps[:, 0:1]).then_inc(n_ln, 1)
                    eng.wait_ge(n_ln, 2 * i + t + 1)
                    eng.activation(rr[:, t], rr[:, t], ACT.Exp, scale=-0.5).then_inc(r_ready, 1)
                eng.wait_ge(sp_ready, i + 1)
                eng.activation(dec[:, hh, b], sp, ACT.Exp, scale=gnegA[:, hh:hh + 1]).then_inc(dec_ready, 1)

            def prep(n, c, p):
                eng.activation(gbi(ks[:, p]), chunk(qkv[:, 1], c), ACT.Copy).then_inc(ks_ready, 1)

            def prep_decays(n, c):
                eng.activation(gbi(es), chunk(dec, c), ACT.Copy).then_inc(es_ready, 1)

            def prep_v(n, c):
                eng.activation(gbi(vs[:, :]), chunk(qkv[:, 2], c), ACT.Copy).then_inc(vs_ready, 1)

            def slot(g, n, c, p, step=True, scan=True, prepare=True):
                m, q = n - 1, 1 - p

                def inverse(l):
                    eng.wait_ge(t_done, (NL - 1) * n + l)
                    if l < NL - 1:
                        eng.activation(half(tmat, LEVELS[l], 0), blocks(bank[3][:, 0:HU], LEVELS[l]), ACT.Copy)
                    eng.activation(half(tt[:, p], LEVELS[l], 1), blocks(bank[3][:, HU:UN], LEVELS[l]),
                                   ACT.Copy).then_inc(t_ready, 1)

                if scan:
                    eng.wait_ge(u_done, n)
                    eng.activation(us, bank[4][:, :], ACT.Copy).then_inc(us_ready, 1)
                if step:
                    inverse(1)
                if scan:
                    eng.wait_ge(o_done, n)
                    eng.activation(osq, bank[5][:, :], ACT.Square).then_inc(osq_ready, 1)
                if step:
                    inverse(2)
                if scan:
                    eng.wait_ge(ssq_ready, n)
                    eng.activation(ssq[:, 1], ssq[:, 0], ACT.Ln, bias=eps[:, 1:2],
                                   scale=SCALE * SCALE / D).then_inc(ssq_ln, 1)
                    eng.wait_ge(ssq_ln, n)
                    eng.activation(ssq[:, 2], ssq[:, 1], ACT.Exp, bias=eps[:, 3:4], scale=-0.5).then_inc(rms_ready, 1)
                if step:
                    inverse(3)
                if step and prepare:
                    eng.wait_ge(vt_done, n + 1)
                    prep_v(n + 1, c + 1)
                if scan:
                    eng.wait_ge(ot_done, n)
                    eng.activation(oT, bank[7][:, :], ACT.Copy).then_inc(ot_ready, 1)
                if step:
                    inverse(4)
                    if prepare:
                        prep(n + 1, c + 1, q)
                        prep_decays(n + 1, c + 1)
                    inverse(5)
                    eng.wait_ge(kst_done, n + 1)
                    eng.activation(kst, bank[7][:, :], ACT.Copy).then_inc(kst_ready, 1)

            with eng.Fori(0, NG) as g:
                n0 = g * NCH
                barrier(eng, act_free, g)
                eng.wait_ge(gprep, g + 1)
                for hh in range(G):
                    for b in range(B):
                        item(g, hh, b)
                eng.wait_ge(conved, 3 * ITEMS * g + 3 * ITEMS)
                for t in (1, 0, 2):
                    v = qkv[:, t].rearrange("p g b s -> p (g b s)")
                    eng.activation(v, v, ACT.Silu).then_inc(silued, 1)
                for c in range(NCH):
                    eng.wait_ge(gate_done, NCH * g + c + 1)
                    eng.activation(gate[:, c], bank[c % 4][:, :], ACT.Tanh, scale=0.5).then_inc(gated, 1)
                eng.wait_ge(silued, 3 * g + 3)
                eng.wait_ge(dec_ready, ITEMS * g + ITEMS)
                prep(n0, 0, 0)
                prep_decays(n0, 0)
                prep_v(n0, 0)
                run_slots(eng, slot, g)
                eng.drain().then_inc(act_free, 1)
            layer_norm(2)
            feed_forward(1)

        @block.tensor
        def _(eng):
            def layer_norm(f):
                eng.wait_ge(ln_ready, f + 1)
                for kt in range(KT):
                    for i in range(2):
                        for c in range(HALF):
                            last = eng.transpose(bank[2 * kt + i][:, c * P:(c + 1) * P],
                                                 hn[:, i * HALF + c, kt * P:(kt + 1) * P], ident[:, :])
                        last.then_inc(ln_tr, 1)
                eng.wait_ge(hT_act, 2 * f + 2)
                eng.wait_ge(hT_dve, 2 * f + 2)

            def feed_forward(j):
                if j == 0:
                    eng.wait_ge(in_ffn, 16 * N_FFN)
                for c in range(NCH):
                    o = bank[4 + c // HALF][:, (c % HALF) * P:]
                    for kt in range(KT):
                        eng.matmul(o[:, 0:RW + E], hT[:, kt, c * P:(c + 1) * P], w_a[:, kt, :],
                                   start=(kt == 0), stop=False)
                    last = eng.matmul(o[:, RW:RW + E], ones[0:1, :], brow[:, :], start=False, stop=True)
                    if c % HALF == HALF - 1:
                        last.then_inc(f_low, 1)
                eng.wait_ge(f_hw, j + 1)
                for c in range(NCH):
                    last = eng.transpose(bank[6 + c // HALF][0:NROW, (c % HALF) * P:(c % HALF + 1) * P],
                                         hw[:, c, :], ident[:, :])
                    if c % HALF == HALF - 1:
                        last.then_inc(f_hwT, 1)
                for c in range(NCH):
                    o = bank[c // 2][:, (c % 2) * HID:(c % 2 + 1) * HID]
                    for kt in range(KT):
                        eng.matmul(o, hT[:, kt, c * P:(c + 1) * P], w_base[:, kt, :], start=(kt == 0), stop=False)
                    if c % HALF == 0:
                        eng.wait_ge(f_hwTs, 2 * j + c // HALF + 1)
                    last = eng.matmul(o, hwT[:, c, :], w_b[:, :], start=False, stop=True)
                    if c % 2:
                        last.then_inc(f_out, 1)

            eng.wait_ge(const_ready, 1)
            eng.wait_ge(in_small, 16 * N_SMALL)
            nrow2 = TAPS * H + H + 1
            eng.transpose(bank[4][:, 0:P], rows1[:, :], ident[:, :])
            eng.transpose(bank[5][:, 0:nrow2], rows2[0:nrow2, :], ident[0:nrow2, 0:nrow2]).then_inc(rows_done, 1)
            eng.wait_ge(chan_ready, 1)
            layer_norm(0)
            feed_forward(0)
            layer_norm(1)
            eng.wait_ge(in_low, 16 * N_LOW)
            for w, o in ((wfa, 4), (wga, 6)):
                for b in range(B):
                    for kt in range(KT):
                        last = eng.matmul(bank[o + b][:, :], w[:, kt, :], hT[:, kt, b * S:(b + 1) * S],
                                          start=(kt == 0), stop=(kt == KT - 1))
                    last.then_inc(low_done, 1)
            for b in range(B):
                for kt in range(KT):
                    eng.matmul(bank[b][0:H, :], wbeta[:, kt, :], hT[:, kt, b * S:(b + 1) * S],
                               start=(kt == 0), stop=(kt == KT - 1))
            for b in range(B):
                for c in range(NCH):
                    for kt in range(KT):
                        last = eng.matmul(bank[2][b * C:(b + 1) * C, c * H:(c + 1) * H],
                                          hT[:, kt, b * S + c * C:b * S + (c + 1) * C],
                                          wbeta[:, kt, :], start=(kt == 0), stop=(kt == KT - 1))
            last.then_inc(beta_done, 1)
            eng.wait_ge(low_copied, 2 * B)
            eng.wait_ge(beta_ready, 1)
            eng.drain().then_inc(pe_free, 1)

            def project(g, hh, b):
                j = hh * B + b
                i = g * ITEMS + j
                cols = slice(hh * D, (hh + 1) * D)
                toks = slice(b * S, (b + 1) * S)
                for t, freed, value, done in ((0, normed, 2 * i - 1, q_done), (1, normed, 2 * i, k_done),
                                              (2, v_copied, i, v_done)):
                    if j:
                        eng.wait_ge(freed, value)
                    for kt in range(KT):
                        last = eng.matmul(bank[t][:, :], gw[:, t, kt, cols], hT[:, kt, toks],
                                          start=(kt == 0), stop=(kt == KT - 1))
                    last.then_inc(done, 1)
                if j:
                    eng.wait_ge(sp_ready, i)
                eng.matmul(bank[3][:, :], gfb[:, cols], faT[:, toks], start=True, stop=True).then_inc(f_done, 1)
                for t in range(2):
                    eng.wait_ge(sq_ready, 2 * i + t + 1)
                    if j:
                        eng.wait_ge(n_ln, 2 * i - 1 + t)
                    eng.matmul(bank[5 + t][:, :], ones[:, :], sq[:, t], start=True, stop=True).then_inc(n_done, 1)

            def slot(g, n, c, p, step=True, scan=True, prepare=True):
                m, q = n - 1, 1 - p

                def level(l):
                    h = LEVELS[l]
                    if l == 0:
                        eng.wait_ge(kq_ready, n + 1)
                    else:
                        eng.wait_ge(updated, NL * n + l)
                    o = bank[l % 2][:, :].rearrange("p (a u t) -> p a u t", a=2, u=G)
                    for u in range(G):
                        last = eng.matmul(o[:, :, u, :].rearrange("p a (n t) -> p a n t", t=h), unit(ks[:, p], u),
                                          half(kq[:, p, :, u * P:(u + 1) * P], h, 1), start=True, stop=True)
                    last.then_inc(level_done, 1)

                def inverse_y(l):
                    h = LEVELS[l]
                    eng.wait_ge(n_ready, NL * n + l + 1)
                    if l == 0:
                        eng.wait_ge(diag_ready, n + 1)
                    elif l == 1:
                        eng.wait_ge(f_ready, NL * n + 1)
                        eng.wait_ge(tt0_ready, n + 1)
                    else:
                        eng.wait_ge(t_ready, (NL - 1) * n + l - 1)
                    for u in range(G):
                        if l == 0:
                            last = eng.matmul(unit(bank[2], u), unit(nmat[:, 0], u), ident[:, :], start=True, stop=True)
                        else:
                            last = eng.matmul(bank[2][:, u * C:(u + 1) * C].rearrange("p (n t) -> p n t", t=h),
                                              unit(nmat[:, l], u), half(unit(tmat, u), h, 0), start=True, stop=True)
                    last.then_inc(y_done, 1)

                def inverse_t(l):
                    h = LEVELS[l]
                    eng.wait_ge(f_ready, NL * n + l + 1)
                    if l < NL - 1:
                        for u in range(G):
                            eng.matmul(bank[3][:, u * C:(u + 1) * C].rearrange("p (n t) -> p n t", t=h),
                                       unit(tt[:, p], u), half(unit(fmat[:, l - 1], u), h, 0), start=True, stop=True)
                    for u in range(G):
                        last = eng.matmul(bank[3][:, HU + u * C:HU + (u + 1) * C].rearrange("p (n t) -> p n t", t=h),
                                          unit(fmat[:, l - 1], u), half(unit(tt[:, p], u), h, 1), start=True, stop=True)
                    last.then_inc(t_done, 1)

                if step:
                    if scan:
                        eng.wait_ge(aq_ready, NL * n)
                    for u in range(G):
                        last = eng.matmul(unit(bank[1], u), gsel[:, u:u + 1].broadcast_to((H, P)),
                                          beta16[:, :].rearrange("p (b t) -> p b t", b=B)[:, :, ds(c * C, C)],
                                          start=True, stop=True)
                    last.then_inc(b_done, 1)
                    eng.wait_ge(ks_ready, n + 1)
                    for u in range(G):
                        last = eng.matmul(unit(bank[2], u), unit(ks[:, p], u), qkv[:, 0, u, :, ds(c * C, C)],
                                          start=True, stop=True)
                    last.then_inc(diag_done, 1)
                    level(0)
                if scan:
                    eng.wait_ge(state_ready, B * m + g + 1)
                    for b in range(B):
                        for u in range(G):
                            last = eng.matmul(unit(bank[4], u)[b * C:(b + 1) * C, :],
                                              kq[:, q, 0, u * P + b * C:u * P + (b + 1) * C],
                                              unit(state[:, b], u), start=True, stop=True)
                    last.then_inc(r_done, 1)
                if step:
                    level(1)
                    inverse_y(0)
                if scan:
                    for b in range(B):
                        for u in range(G):
                            eng.matmul(unit(bank[5], u)[b * C:(b + 1) * C, :],
                                       kq[:, q, 1, u * P + b * C:u * P + (b + 1) * C],
                                       unit(state[:, b], u), start=(u == 0), stop=False, skip_group_check=True)
                    eng.wait_ge(rs_ready, n)
                    eng.wait_ge(t_ready, (NL - 1) * n)
                    for u in range(G):
                        last = eng.matmul(unit(bank[4], u), unit(tt[:, q], u), unit(rs, u), start=True, stop=True)
                    last.then_inc(u_done, 1)
                if step:
                    level(2)
                    inverse_y(1)
                if scan:
                    eng.wait_ge(us_ready, n)
                    eng.wait_ge(aq_ready, NL * n)
                    for u in range(G):
                        last = eng.matmul(unit(bank[5], u), unit(aq[:, q], u), unit(us, u), start=False, stop=True,
                                          skip_group_check=True)
                    last.then_inc(o_done, 1)

                def state_add(b):
                    rows = slice(b * C, (b + 1) * C)
                    for u in range(G):
                        last = eng.matmul(unit(bank[6], u), unit(kst, u)[rows, :], unit(us, u)[rows, :],
                                          start=True, stop=True)
                    last.then_inc(s_done, 1)

                if scan:
                    eng.wait_ge(kst_ready, n)
                    state_add(0)
                if step:
                    inverse_t(1)
                    level(3)
                    inverse_y(2)
                if scan:
                    eng.wait_ge(state_ready, B * m + g + 2)
                    state_add(1)
                if step:
                    inverse_t(2)
                    eng.wait_ge(vs_ready, n + 1)
                    for u in range(G):
                        last = eng.transpose(unit(bank[7], u), unit(vs, u), ident[:, :])
                    last.then_inc(vt_done, 1)
                    level(4)
                    inverse_y(3)
                    inverse_t(3)
                    level(5)
                    inverse_y(4)
                if scan:
                    if step:
                        eng.wait_ge(vb_ready, n + 1)
                    eng.wait_ge(on_ready, n)
                    for u in range(G):
                        last = eng.transpose(unit(bank[7], u), unit(og, u), ident[:, :])
                    last.then_inc(ot_done, 1)
                if step:
                    inverse_t(4)
                    inverse_y(5)
                if scan:
                    eng.wait_ge(ot_ready, n)
                    for u in range(G):
                        last = eng.matmul(bank[7][:, 0:HID], unit(oT, u), gwo[:, u, :], start=(u == 0), stop=(u == G - 1))
                    last.then_inc(wo_done, 1)
                if step:
                    inverse_t(5)
                    eng.wait_ge(updated, NL * n + NL)
                    if scan:
                        eng.wait_ge(x_added, n)
                    else:
                        eng.wait_ge(vb_ready, n + 1)
                    for u in range(G):
                        last = eng.transpose(unit(bank[7], u), unit(ks[:, p], u), ident[:, :])
                    last.then_inc(kst_done, 1)

            with eng.Fori(0, NG) as g:
                barrier(eng, pe_free, g)
                eng.wait_ge(in_group, 16 * N_GROUP * g + 16 * N_GROUP)
                eng.wait_ge(gprep, g + 1)
                for hh in range(G):
                    for b in range(B):
                        project(g, hh, b)
                last_item = ITEMS * g + ITEMS
                eng.wait_ge(normed, 2 * last_item)
                eng.wait_ge(v_copied, last_item)
                eng.wait_ge(sp_ready, last_item)
                for c in range(NCH):
                    if c >= 4:
                        eng.wait_ge(gated, NCH * g + c - 3)
                    eng.matmul(bank[c % 4][:, :], gaT[:, c].rearrange("p b i -> p (b i)"), ggb[:, :],
                               start=True, stop=True).then_inc(gate_done, 1)
                eng.wait_ge(n_ln, 2 * last_item)
                eng.wait_ge(gated, NCH * g + NCH)
                eng.wait_ge(silued, 3 * g + 3)
                eng.wait_ge(wos_ready, g + 1)
                run_slots(eng, slot, g)
                eng.drain().then_inc(pe_free, 1)
            layer_norm(2)
            feed_forward(1)

        @block.vector
        def _(eng):
            chain = [0]

            def link(ins):
                chain[0] += 1
                ins.then_inc(dve_chain, 1)
                eng.wait_ge(dve_chain, chain[0])

            def layer_norm(f):
                link(eng.tensor_reduce(st[:, 0], x[:, :, :], AX.X, ALU.add))
                link(eng.tensor_scalar(st[:, 1], st[:, 0], 1.0 / HID, None, ALU.mult))
                eng.tensor_tensor(hn, x[:, :, :], spread(st[:, 1], HID), ALU.subtract).then_inc(ln_centred, 1)
                eng.wait_ge(ln_rstd, f + 1)
                eng.tensor_tensor(hn, hn, spread(st[:, 4], HID), ALU.mult).then_inc(ln_ready, 1)
                for i in range(2):
                    eng.wait_ge(ln_tr, 4 * f + 2 + i + 1)
                    eng.tensor_copy(*move_hT(f, 1, i)).then_inc(hT_dve, 1)

            def feed_forward(j):
                low = [bank[4 + i][:, :].rearrange("p (c r) -> p c r", c=HALF) for i in range(2)]
                tiles = [slice(i * HALF, (i + 1) * HALF) for i in range(2)]
                for i in range(2):
                    eng.wait_ge(f_low, 2 * j + i + 1)
                    last = eng.tensor_copy(lg[:, tiles[i], :], low[i][:, :, RW:RW + E])
                link(last)
                link(eng.tensor_reduce(sm[:, 0], lg[:, :, :], AX.X, ALU.max))
                eng.tensor_tensor(lg[:, :, :], lg[:, :, :], spread(sm[:, 0], E), ALU.subtract).then_inc(f_sub, 1)
                eng.wait_ge(f_exp, j + 1)
                link(eng.tensor_reduce(sm[:, 1], gt[:, :, :], AX.X, ALU.add))
                link(eng.reciprocal(sm[:, 2], sm[:, 1]))
                link(eng.tensor_tensor(gt[:, :, :], gt[:, :, :], spread(sm[:, 2], E), ALU.mult))
                for e in range(E):
                    o = rk if e == 0 else beats
                    ge = gt[:, :, e:e + 1]
                    last = eng.tensor_tensor(o[:, :, 0:e + 1], ge.broadcast_to((P, NCH, e + 1)), gt[:, :, 0:e + 1], ALU.is_gt)
                    if e < E - 1:
                        last = eng.tensor_tensor(o[:, :, e + 1:E], ge.broadcast_to((P, NCH, E - 1 - e)),
                                                 gt[:, :, e + 1:E], ALU.is_ge)
                    link(last)
                    if e:
                        link(eng.tensor_tensor(rk[:, :, :], rk[:, :, :], beats[:, :, :], ALU.add))
                link(eng.scalar_tensor_tensor(out=gt[:, :, :], in0=rk[:, :, :], scalar=float(TOP), in1=gt[:, :, :],
                                              op0=ALU.is_lt, op1=ALU.mult))
                eng.memset(hw[:, :, RW:NROW], 1.0)
                for i in range(2):
                    eng.tensor_copy(hw[:, tiles[i], 0:R], low[i][:, :, 0:R])
                    last = eng.tensor_tensor(
                        hw[:, tiles[i], R:RW].rearrange("p c (e r) -> p c e r", e=E),
                        low[i][:, :, R:RW].rearrange("p c (e r) -> p c e r", e=E),
                        gt[:, tiles[i], :].rearrange("p c (e o) -> p c e o", o=1).broadcast_to((P, HALF, E, R)), ALU.mult)
                last.then_inc(f_hw, 1)
                for i in range(NCH // 2):
                    eng.wait_ge(f_out, NCH // 2 * j + i + 1)
                    v = x[:, 2 * i:2 * i + 2, :].rearrange("p c d -> p (c d)")
                    last = eng.scalar_tensor_tensor(out=v, in0=bank[i][:, :], scalar=0.5, in1=v, op0=ALU.mult, op1=ALU.add)
                last.then_inc(x_ready, 1)
                eng.wait_ge(x_ready, j + 1)

            eng.wait_ge(rows_done, 1)
            flat = chan[:, :, :].rearrange("p r h -> p (r h)")
            nrow2 = TAPS * H + H
            eng.tensor_copy(flat[:, 0:P], bank[4][:, 0:P])
            eng.tensor_copy(flat[:, P:P + nrow2], bank[5][:, 0:nrow2])
            eng.tensor_copy(rmsc[:, :], bank[5][:, nrow2:nrow2 + 1]).then_inc(chan_ready, 1)
            eng.wait_ge(in_x, 16 * B)
            layer_norm(0)
            feed_forward(0)
            layer_norm(1)
            eng.wait_ge(beta_exp, 1)
            link(eng.tensor_scalar(beta16[:, :], beta16[:, :], 1.0, None, ALU.add))
            eng.reciprocal(beta16[:, :], beta16[:, :])
            link(eng.tensor_scalar(btok[:, :, :], btok[:, :, :], 1.0, None, ALU.add))
            eng.reciprocal(btok[:, :, :], btok[:, :, :]).then_inc(beta_ready, 1)
            eng.wait_ge(chan_ready, 1)
            eng.wait_ge(nega_ready, 1)
            eng.wait_ge(beta_ready, 1)
            eng.drain().then_inc(dve_free, 1)

            def item(g, hh, b):
                j = hh * B + b
                i = g * ITEMS + j
                steps = [0]
                bias = gchan[:, DT, hh:hh + 1]
                eng.wait_ge(f_done, i + 1)
                if j:
                    eng.wait_ge(z_ln, i)
                eng.tensor_scalar(zc, bank[3][:, :], bias, SOFT_MAX, ALU.add, ALU.min).then_inc(z_ready, 1)

                def conv(t):
                    o = qkv[:, t, hh, b, :]
                    for tap in range(TAPS):
                        src = pad[:, t, tap:tap + S]
                        w = gchan[:, t * TAPS + tap, hh:hh + 1]
                        if tap == 0:
                            last = eng.tensor_scalar(o, src, w, None, ALU.mult)
                        else:
                            eng.wait_ge(conv_chain, 3 * (TAPS - 1) * i + steps[0])
                            last = eng.scalar_tensor_tensor(out=o, in0=src, scalar=w, in1=o, op0=ALU.mult, op1=ALU.add)
                        if tap < TAPS - 1:
                            steps[0] += 1
                            last.then_inc(conv_chain, 1)
                    last.then_inc(conved, 1)

                eng.wait_ge(v_copied, i + 1)
                conv(2)
                eng.wait_ge(z_ln, i + 1)
                eng.scalar_tensor_tensor(out=sp, in0=bank[3][:, :], scalar=bias, in1=sp,
                                         op0=ALU.add, op1=ALU.max).then_inc(sp_ready, 1)
                for t in range(2):
                    eng.wait_ge(r_ready, 2 * i + t + 1)
                    eng.tensor_tensor(pad[:, t, TAPS - 1:], bank[t][:, :], rr[:, t], ALU.mult).then_inc(normed, 1)
                for t in range(2):
                    eng.wait_ge(normed, 2 * i + t + 1)
                    conv(t)

            def slot(g, n, c, p, step=True, scan=True, prepare=True):
                m, q = n - 1, 1 - p

                def level(l):
                    h = LEVELS[l]
                    lower, upper = (tots[l].rearrange("p (n t) -> p n t", t=2)[:, :, i] for i in range(2))
                    nb = HU // h
                    if l:
                        eng.wait_ge(aq_ready, NL * n + l)
                    else:
                        eng.wait_ge(diag_ready, n + 1)
                    eng.wait_ge(level_done, NL * n + l + 1)
                    eng.tensor_tensor(half(kq[:, p], h, 1), half(kq[:, p], h, 1),
                                      lower.rearrange("p (a n o) -> p a n o", a=1, o=1).broadcast_to((P, 2, nb, h)), ALU.mult)
                    eng.tensor_tensor(half(ks[:, p], h, 0), half(ks[:, p], h, 0), spread(upper, h), ALU.mult)
                    eng.tensor_tensor(tots[l + 1] if l < NL - 1 else gamma[:, p], lower, upper, ALU.mult).then_inc(updated, 1)

                def inverse(l):
                    h = LEVELS[l]
                    eng.wait_ge(y_done, NL * n + l + 1)
                    if l == 0:
                        eng.tensor_tensor(gd(tmat), ident4, gd(bank[2][:, :]), ALU.subtract).then_inc(f_ready, 1)
                    else:
                        lower = [v.rearrange("p u (n t) -> p u n t", t=2 * h)[:, :, :, 0:h] for v in (gd(fmat[:, l - 1]), ident4)]
                        eng.tensor_tensor(lower[0], lower[1],
                                          bank[2][:, 0:HU].rearrange("p (u n t) -> p u n t", u=G, t=h),
                                          ALU.subtract).then_inc(f_ready, 1)

                def keep(l):
                    h = LEVELS[l]
                    mask = blocks(masks[:, l], h)
                    eng.copy_predicated(half(nmat[:, l], h, 1), mask, blocks(bank[l % 2][:, 0:HU], h)).then_inc(n_ready, 1)
                    eng.copy_predicated(half(aq[:, p], h, 1), mask, blocks(bank[l % 2][:, HU:UN], h)).then_inc(aq_ready, 1)

                if step:
                    eng.wait_ge(b_done, n + 1)
                    eng.tensor_tensor(gbi(kq[:, p, 0]), chunk(qkv[:, 1], c), gbi(bank[1][:, :]), ALU.mult).then_inc(kb_ready, 1)
                    eng.wait_ge(es_ready, n + 1)
                    eng.tensor_tensor(gbi(kq[:, p, 1]), chunk(qkv[:, 0], c), gbi(es), ALU.mult)
                    eng.wait_ge(kb_ready, n + 1)
                    eng.tensor_tensor(kq[:, p, 0], kq[:, p, 0], es, ALU.mult).then_inc(kq_ready, 1)
                    eng.wait_ge(diag_done, n + 1)
                    eng.tensor_tensor(gd(aq[:, p]), gd(bank[2][:, :]), ident4, ALU.mult).then_inc(diag_ready, 1)
                    level(0)
                    keep(0)
                if scan:
                    eng.wait_ge(r_done, n)
                    eng.wait_ge(vb_ready, n)
                    eng.tensor_tensor(rs, vb, bank[4][:, :], ALU.subtract).then_inc(rs_ready, 1)
                if step:
                    level(1)
                    inverse(0)
                    keep(1)
                    level(2)
                    inverse(1)
                    keep(2)

                def add_state(b):
                    eng.wait_ge(s_done, B * m + b + 1)
                    eng.tensor_tensor(state[:, b], sdec[:, b], bank[6][:, :], ALU.add).then_inc(state_ready, 1)

                if scan:
                    eng.wait_ge(sdec_ready, n)
                    add_state(0)
                if step:
                    level(3)
                    inverse(2)
                    keep(3)
                if scan:
                    add_state(1)
                    eng.wait_ge(osq_ready, n)
                    eng.tensor_reduce(ssq[:, 0], gd(osq), AX.X, ALU.add).then_inc(ssq_ready, 1)
                    eng.scalar_tensor_tensor(out=og, in0=gate[:, ds(c - 1, 1), :].rearrange("p a d -> p (a d)"),
                                             scalar=1.0, in1=bank[5][:, :], op0=ALU.add, op1=ALU.mult).then_inc(og_ready, 1)
                if step:
                    eng.wait_ge(vt_done, n + 1)
                    eng.tensor_tensor(gd(vb), gd(bank[7][:, :]),
                                      spread(btok[:, ds(c, 1), ds(g * G, G)].rearrange("p a h -> p (a h)"), D),
                                      ALU.mult).then_inc(vb_ready, 1)
                    level(4)
                    inverse(3)
                    keep(4)
                    level(5)
                    inverse(4)
                    keep(5)
                    inverse(5)
                if scan:
                    eng.wait_ge(wo_done, n)
                    v = x[:, ds(c - 1, 1), :].rearrange("p a d -> p (a d)")
                    eng.tensor_tensor(v, v, bank[7][:, 0:HID], ALU.add).then_inc(x_added, 1)

            with eng.Fori(0, NG) as g:
                barrier(eng, dve_free, g)
                heads = ds(g * G, G)
                eng.memset(pad[:, :, 0:TAPS - 1], 0.0)
                eng.tensor_copy(gchan[:, :, :], chan[:, :, heads])
                eng.tensor_copy(gnegA[:, :], negA[:, heads])
                eng.tensor_copy(gsel[:, :], ident[0:H, heads]).then_inc(gprep, 1)
                eng.memset(state[:, :, :], 0.0).then_inc(state_ready, 1)
                eng.wait_ge(in_wo, 16 * g + 16)
                eng.tensor_scalar(gwo[:, :, :], gwo[:, :, :], rmsc[:, :], 0.5, ALU.mult, ALU.mult).then_inc(wos_ready, 1)
                eng.wait_ge(gprep, g + 1)
                for hh in range(G):
                    for b in range(B):
                        item(g, hh, b)
                eng.wait_ge(silued, 3 * g + 3)
                eng.wait_ge(gated, NCH * g + NCH)
                run_slots(eng, slot, g)
                eng.drain().then_inc(dve_free, 1)
            layer_norm(2)
            feed_forward(1)


_PRE = {"L0_attn_hidden_states": "x"}
_INS = ["L0_attn_hidden_states", "L0_attn_Wq", "L0_attn_Wk", "L0_attn_Wv", "L0_attn_conv_q", "L0_attn_conv_k",
        "L0_attn_conv_v", "L0_attn_Wb", "L0_attn_Wfa", "L0_attn_Wfb", "L0_attn_Wga", "L0_attn_Wgb", "L0_attn_A_log",
        "L0_attn_dt_bias", "L0_attn_rms_scale", "L0_attn_Wo", "L0_ffn_W_base", "L0_ffn_b_base", "L0_ffn_A_s",
        "L0_ffn_B_s", "L0_ffn_A_r", "L0_ffn_B_r", "L0_ffn_W_router", "L0_ffn_b_router"]


def kernel(**inputs):
    import numpy as _np
    import concourse.bacc as _bacc
    from concourse import mybir as _mybir
    from concourse.bass_utils import run_bass_kernel_spmd as _run

    nc = _bacc.Bacc("TRN2", target_bir_lowering=False, num_devices=1)
    arrays, aps = {}, {}
    for name in _INS:
        v = _np.ascontiguousarray(inputs[name])
        arrays[f"in_{name}"] = v
        short = _PRE.get(name) or name.split("_", 2)[2]
        aps[short] = nc.dram_tensor(f"in_{name}", v.shape, _mybir.dt.from_np(v.dtype), kind="ExternalInput").ap()
    out = nc.dram_tensor("out", (B, S, HID), F32, kind="ExternalOutput").ap()
    build(nc, aps, out)
    r = _run(nc, [arrays], core_ids=[0])
    return r.results[0]["out"]
```

```python
from contextlib import ExitStack

import numpy as np
import concourse.bass as bass
from concourse import mybir

ALU = mybir.AluOpType
ACT = mybir.ActivationFunctionType
F32 = mybir.dt.float32
U8 = mybir.dt.uint8
AX = mybir.AxisListType
ds = bass.ds

P = 128
B, S, HID = 2, 512, 256
H, D = 16, 128
TAPS = 4
E, R, TOP = 6, 16, 2
T = B * S
C = 64
NCH = S // C
KT = HID // P
G = 4
NG = H // G
UN = G * P
HU = UN // 2
LEVELS = [1 << l for l in range(C.bit_length() - 1)]
NL = len(LEVELS)
LN_EXP = "natural_log_exp_and_others"
SILU_TANH = "silu_and_others"
EPS_L2, EPS_RMS, EPS_LN = 1e-6, 1e-5, 1e-5
SCALE = float(D) ** -0.5
SOFT_MAX = 40.0
RW = (1 + E) * R
NROW = RW + 1
DT = 3 * TAPS
ITEMS = G * B
HALF = NCH // 2
GATE_BANKS = (4, 6)


def build(nc, a, out):
    ctx = ExitStack()
    with ctx:
        def sb(name, shape):
            return ctx.enter_context(nc.sbuf_tensor(name, shape, F32))

        def sems(names):
            return [ctx.enter_context(nc.semaphore(x)) for x in names.split()]

        bank = [ctx.enter_context(nc.psum_tensor(f"bank{i}", [P, 512], F32)) for i in range(8)]

        ident = sb("ident", [P, P])
        ident4 = ident[:, :].rearrange("p (o i) -> p o i", o=1).broadcast_to((P, G, P))
        ones = sb("ones", [P, P])
        masks = ctx.enter_context(nc.sbuf_tensor("masks", [P, NL, HU], U8))
        eps = sb("eps", [P, 2])
        region = sb("region", [P, 10 * UN])

        def part(k, n=1):
            return region[:, k * UN:(k + n) * UN]

        rows1 = part(0)[:, 0:P]
        rows2 = part(0)[:, P:2 * P]
        junk = part(1, 4).rearrange("p (c d) -> p c d", c=NCH)
        sq = part(0, 2).rearrange("p (a s) -> p a s", a=2)
        rr = part(2, 2).rearrange("p (a s) -> p a s", a=2)
        zc = part(4)
        sp = part(5)
        PADW = TAPS - 1 + S
        pad = region[:, 6 * UN:6 * UN + 2 * PADW].rearrange("p (a s) -> p a s", a=2)
        rs, us, osq, og = (part(k) for k in range(4))
        oT = osq
        sdec = part(4, 2).rearrange("p (b s) -> p b s", b=B)
        kst = part(6)
        vb = part(7)
        tmat = part(8)
        es = part(9)
        chan = sb("chan", [P, DT + 1, H])
        rmsc = sb("rmsc", [P, 1])
        negA = sb("negA", [P, H])
        gchan = sb("gchan", [P, DT + 1, G])
        gnegA = sb("gnegA", [P, G])
        w_a = sb("w_a", [P, KT, RW + E])
        w_b = sb("w_b", [NROW, HID])
        w_base = sb("w_base", [P, KT, HID])
        brow = sb("brow", [1, E])
        x = sb("x", [P, NCH, HID])
        gate = sb("gate", [P, NCH, G * D])
        flat_gate = gate[:, :, :].rearrange("p c d -> p (c d)")
        hn = flat_gate[:, 0:NCH * HID].rearrange("p (c d) -> p c d", c=NCH)
        hw = flat_gate[:, NCH * HID:NCH * (HID + NROW)].rearrange("p (c r) -> p c r", c=NCH)
        hwT = flat_gate[0:NROW, NCH * (HID + NROW):NCH * (HID + NROW + P)].rearrange("p (c r) -> p c r", c=NCH)
        hT = sb("hT", [P, KT, T])
        st = sb("st", [P, 5, NCH])
        lg = sb("lg", [P, NCH, E])
        gt = sb("gt", [P, NCH, E])
        rk = sb("rk", [P, NCH, E])
        beats = sb("beats", [P, NCH, E])
        sm = sb("sm", [P, 3, NCH])
        faT = sb("faT", [P, T])
        gaT = sb("gaT", [P, NCH, B, C])
        beta16 = sb("beta16", [H, T])
        btok = sb("btok", [P, NCH, H])
        gw = sb("gw", [P, 3, KT, G * D])
        gfb = sb("gfb", [P, G * D])
        ggb = sb("ggb", [P, G * D])
        gwo = sb("gwo", [P, G, HID])
        gsel = sb("gsel", [H, G])
        qkv = sb("qkv", [P, 3, G, B, S])
        flat_q = qkv[:, 0].rearrange("p g b s -> p (g b s)")
        wfa, wga = (flat_q[:, i * KT * D:(i + 1) * KT * D].rearrange("p (k r) -> p k r", k=KT) for i in range(2))
        wbeta = flat_q[:, 2 * KT * D:2 * KT * D + KT * H].rearrange("p (k r) -> p k r", k=KT)
        fmasks = qkv[:, 1].rearrange("p g b s -> p (g b s)")[:, 0:NL * HU].rearrange("p (l n) -> p l n", l=NL)
        dec = sb("dec", [P, G, B, S])
        kq = sb("kq", [P, 2, 2, UN])
        vtap = [kq[:, 0, 0], kq[:, 0, 1], kq[:, 1, 0]]
        ks = sb("ks", [P, 2, UN])
        qs = sb("qs", [P, UN])
        vs = qs
        tots = [es] + [sb(f"tot{h}", [P, UN // h])[:, :] for h in LEVELS[1:]]
        gamma = sb("gamma", [P, 2, UN // C])
        nmat = sb("nmat", [P, NL, UN])
        fmat = sb("fmat", [P, NL - 1, UN])
        tt = sb("tt", [P, 2, UN])
        aq = sb("aq", [P, 2, UN])
        state = sb("state", [P, B, UN])
        ssq = sb("ssq", [P, 3, G])
        mhalf = sb("mhalf", [P, G])
        eps_sum = sb("eps_sum", [P, G])

        in_x, in_small, in_ffn, in_low, in_group, in_wo, stored = sems("in_x in_small in_ffn in_low in_group in_wo stored")
        const_ready, ident_ready, pool_chain, dve_chain, act_chain = sems("const_ready ident_ready pool_chain dve_chain act_chain")
        rows_done, chan_ready, nega_ready = sems("rows_done chan_ready nega_ready")
        ln_centred, ln_rstd, ln_ready, ln_tr, hT_act, hT_dve = sems("ln_centred ln_rstd ln_ready ln_tr hT_act hT_dve")
        f_low, f_sub, f_exp, f_hw, f_hwT, f_hwTs, f_out, x_ready = sems("f_low f_sub f_exp f_hw f_hwT f_hwTs f_out x_ready")
        low_done, low_copied, beta_done, beta_exp, beta_ready, beta_turned, beta_copied = sems("low_done low_copied beta_done beta_exp beta_ready beta_turned beta_copied")
        pe_free, dve_free, act_free, pool_free = sems("pe_free dve_free act_free pool_free")
        gprep, wos_ready, state_zero = sems("gprep wos_ready state_zero")
        q_done, k_done, v_done, f_done, b_done, n_done = sems("q_done k_done v_done f_done b_done n_done")
        sq_ready, z_ready, z_exp, z_ln, sp_ready, dec_ready = sems(
            "sq_ready z_ready z_exp z_ln sp_ready dec_ready")
        n_ln, r_ready, normed, conv_chain, conved, v_taps, v_chain, gate_done, gated = sems(
            "n_ln r_ready normed conv_chain conved v_taps v_chain gate_done gated")
        kb_ready, es_ready, ks_ready, qs_ready, vs_ready, qk_ready, kq_ready = sems(
            "kb_ready es_ready ks_ready qs_ready vs_ready qk_ready kq_ready")
        diag_done, diag_ready, level_done, updated, n_ready, aq_ready = sems(
            "diag_done diag_ready level_done updated n_ready aq_ready")
        y_done, f_ready, tm_done, tm_ready, tt_done, tt_ready, tt0_ready = sems("y_done f_ready tm_done tm_ready tt_done tt_ready tt0_ready")
        vt_done, vb_ready, kst_done, kst_ready = sems("vt_done vb_ready kst_done kst_ready")
        r_done, rs_ready, u_done, us_ready, o_done = sems("r_done rs_ready u_done us_ready o_done")
        sdec_ready, s_done, state_ready = sems("sdec_ready s_done state_ready")
        osq_ready, ssq_ready, rms_chain, og_ready, on_ready = sems(
            "osq_ready ssq_ready rms_chain og_ready on_ready")
        ot_done, ot_ready, wo_done, x_added = sems("ot_done ot_ready wo_done x_added")

        block = ctx.enter_context(nc.Block())

        def by_batch(ap):
            return [ap[b].rearrange("(c i) d -> i c d", i=C) for b in range(B)]

        def chunk(buf, c):
            return buf[:, :, :, ds(c * C, C)]

        def gbi(ap):
            return ap.rearrange("p (g b i) -> p g b i", g=G, b=B)

        def gd(ap):
            return ap.rearrange("p (g d) -> p g d", g=G)

        def half(ap, h, upper):
            if len(ap.shape) == 3:
                return ap.rearrange("p a (n t) -> p a n t", t=2 * h)[:, :, :, upper * h:upper * h + h]
            return ap.rearrange("p (n t) -> p n t", t=2 * h)[:, :, upper * h:upper * h + h]

        def blocks(ap, h):
            return ap.rearrange("p (n t) -> p n t", t=h)

        def unit(ap, u):
            return ap[:, u * P:(u + 1) * P]

        def spread(ap, n):
            return ap.rearrange("p (m o) -> p m o", o=1).broadcast_to((ap.shape[0], ap.shape[1], n))

        N_FFN = 8 + KT - 1
        N_SMALL = 6
        N_LOW = 3
        N_GROUP = 5

        @block.sync
        def _(eng):
            for b in range(B):
                eng.dma_start(x[b * C:(b + 1) * C, :, :], by_batch(a["x"])[b]).then_inc(in_x, 16)
            for dst, src in (
                    (w_a[:, :, 0:R], a["A_s"].rearrange("(k p) r -> p k r", p=P)),
                    *((w_a[:, k, R:RW].rearrange("p (e r) -> p e r", e=E),
                       a["A_r"][:, k * P:(k + 1) * P, :].rearrange("e p r -> p e r")) for k in range(KT)),
                    (w_a[:, :, RW:RW + E], a["W_router"].rearrange("(k p) r -> p k r", p=P)),
                    (brow[:, :], a["b_router"].rearrange("(a e) -> a e", a=1)),
                    (w_b[0:R, :], a["B_s"]),
                    (w_b[R:RW, :], a["B_r"].rearrange("e r d -> (e r) d")),
                    (w_b[RW:NROW, :], a["b_base"].rearrange("(a e) -> a e", a=1)),
                    (w_base[:, :, :], a["W_base"].rearrange("(k p) r -> p k r", p=P))):
                eng.dma_start(dst, src).then_inc(in_ffn, 16)
            TH = TAPS * H
            for dst, src in (
                    (rows1[0:TH, :], a["conv_q"].rearrange("t o (h d) -> (t o h) d", d=D)),
                    (rows1[TH:2 * TH, :], a["conv_k"].rearrange("t o (h d) -> (t o h) d", d=D)),
                    (rows2[0:TH, :], a["conv_v"].rearrange("t o (h d) -> (t o h) d", d=D)),
                    (rows2[TH:TH + H, :], a["dt_bias"].rearrange("(h d) -> h d", d=D)),
                    (rows2[TH + H:TH + H + 1, :], a["rms_scale"].rearrange("(a d) -> a d", a=1)),
                    (negA[:, :], a["A_log"].rearrange("a b h c -> (a b c) h").broadcast_to((P, H)))):
                eng.dma_start(dst, src).then_inc(in_small, 16)
            for dst, src in ((wfa, a["Wfa"]), (wga, a["Wga"]), (wbeta, a["Wb"])):
                eng.dma_start(dst, src.rearrange("(k p) r -> p k r", p=P)).then_inc(in_low, 16)

            def group_weights(g):
                cols = ds(g * (G * D), G * D)
                for i, w in enumerate(("Wq", "Wk", "Wv")):
                    eng.dma_start(gw[:, i], a[w].rearrange("(k p) r -> p k r", p=P)[:, :, cols]).then_inc(in_group, 16)
                eng.dma_start(gfb[:, :], a["Wfb"][:, cols]).then_inc(in_group, 16)
                eng.dma_start(ggb[:, :], a["Wgb"][:, cols]).then_inc(in_group, 16)

            def output_weights(g):
                eng.dma_start(gwo[:, :, :],
                              a["Wo"].rearrange("(h p) n -> p h n", p=P)[:, ds(g * G, G), :]).then_inc(in_wo, 16)

            group_weights(0)
            output_weights(0)
            with eng.Fori(1, NG) as g:
                eng.wait_ge(gate_done, NCH * g)
                group_weights(g)
                eng.wait_ge(pe_free, g + 1)
                output_weights(g)
            eng.wait_ge(x_ready, 2)
            for b in range(B):
                eng.dma_start(by_batch(out)[b], x[b * C:(b + 1) * C, :, :]).then_inc(stored, 16)
            eng.wait_ge(stored, 16 * B)

        def move_hT(f, kt, i):
            src = bank[2 * kt + i]
            if f == 1:
                return (hT[:, kt].rearrange("p (b c i) -> p c b i", b=B, c=NCH)[:, i * HALF:(i + 1) * HALF],
                        src[:, :].rearrange("p (c b i) -> p c b i", b=B, c=HALF))
            return hT[:, kt, i * 512:(i + 1) * 512], src[:, :]

        def run_slots(eng, slot, g):
            n0 = g * NCH
            slot(g, n0, 0, 0, scan=False)
            with eng.Fori(0, NCH // 2 - 1) as w:
                slot(g, n0 + 2 * w + 1, 2 * w + 1, 1)
                slot(g, n0 + 2 * w + 2, 2 * w + 2, 0)
            slot(g, n0 + NCH - 1, NCH - 1, 1, following=False)
            slot(g, n0 + NCH, NCH, 0, step=False, following=False)

        def barrier(eng, own, g):
            for s in (pe_free, dve_free, act_free, pool_free):
                if s is not own:
                    eng.wait_ge(s, g + 1)

        @block.gpsimd
        def _(eng):
            eng.memset(ones[:, :], 1.0)
            for i, v in enumerate((EPS_L2, EPS_LN)):
                eng.memset(eps[:, i:i + 1], v)
            eng.memset(mhalf[:, :], -0.5)
            eng.memset(eps_sum[:, :], EPS_RMS * D / (SCALE * SCALE))
            eng.memset(ident[:, :], 0.0).then_inc(pool_chain, 1)
            eng.wait_ge(pool_chain, 1)
            eng.affine_select(out=ident[:, :], in_=ident[:, :], compare_op=ALU.not_equal, fill=1.0,
                              base=0, pattern=[[-1, P]], channel_multiplier=1).then_inc(ident_ready, 1)
            eng.memset(fmasks, 1.0)
            eng.memset(nmat[:, :, :], 0.0).then_inc(pool_chain, 1)
            eng.wait_ge(pool_chain, 2)

            def level_mask(l, base, step, mult):
                h = LEVELS[l]
                v = fmasks[:, l, :].rearrange("p (u n t) -> p u n t", u=G, t=h)
                return eng.affine_select(out=v, in_=v, compare_op=ALU.is_ge, fill=0.0, base=base,
                                         pattern=[[0, G], [step, P // (2 * h)], [0, h]], channel_multiplier=mult)

            for l, h in enumerate(LEVELS):
                last = level_mask(l, 0, -2 * h, 1)
            last.then_inc(pool_chain, 1)
            eng.wait_ge(pool_chain, 3)
            for l, h in enumerate(LEVELS):
                level_mask(l, h - 1, 2 * h, -1)
            for l in range(1, NL):
                last = eng.tensor_copy(gd(fmat[:, l - 1]), ident4)
            last.then_inc(pool_chain, 1)
            eng.wait_ge(pool_chain, 4)
            eng.tensor_copy(masks[:, :, :], fmasks).then_inc(const_ready, 1)
            eng.drain().then_inc(pool_free, 1)

            def slot(g, n, c, p, step=True, scan=True, following=True):
                m, q = n - 1, 1 - p
                if step:
                    eng.wait_ge(n_ready, NL * n + 1)
                    eng.tensor_tensor(gd(tt[:, p]), ident4, gd(nmat[:, 0]), ALU.subtract).then_inc(tt0_ready, 1)
                if scan:
                    eng.wait_ge(state_ready, B * m + g + 1)
                    eng.wait_ge(updated, NL * n)
                    for b in range(B):
                        decay = gamma[:, q].rearrange("p (g b) -> p b g", b=B)[:, b, :]
                        eng.tensor_tensor(gd(sdec[:, b]), gd(state[:, b]), spread(decay, D), ALU.mult).then_inc(sdec_ready, 1)
                    eng.wait_ge(ssq_ready, n)
                    eng.tensor_tensor(ssq[:, 1], ssq[:, 0], eps_sum[:, :], ALU.add).then_inc(rms_chain, 1)
                    eng.wait_ge(rms_chain, 2 * n - 1)
                    eng.tensor_tensor(ssq[:, 2], ssq[:, 1], mhalf[:, :], ALU.pow).then_inc(rms_chain, 1)
                    eng.wait_ge(rms_chain, 2 * n)
                    eng.wait_ge(og_ready, n)
                    eng.tensor_tensor(gd(og), gd(og), spread(ssq[:, 2, :], D), ALU.mult).then_inc(on_ready, 1)
                if following:
                    head(n + 1, q)

            def head(n, p):
                eng.wait_ge(ks_ready, n + 1)
                eng.wait_ge(qs_ready, n + 1)
                eng.tensor_tensor(kq[:, p, 1], ks[:, p], qs[:, :], ALU.mult).then_inc(qk_ready, 1)

            with eng.Fori(0, NG) as g:
                barrier(eng, pool_free, g)
                for hh in range(G):
                    for b in range(B):
                        i = g * ITEMS + hh * B + b
                        eng.wait_ge(v_taps, i + 1)
                        for tap in range(TAPS - 1):
                            shift = TAPS - 1 - tap
                            o = qkv[:, 2, hh, b, shift:]
                            if tap:
                                eng.wait_ge(v_chain, (TAPS - 1) * i + tap)
                            eng.tensor_tensor(o, o, vtap[tap][:, 0:S - shift], ALU.add).then_inc(v_chain, 1)
                head(g * NCH, 0)
                run_slots(eng, slot, g)
                eng.drain().then_inc(pool_free, 1)

        @block.scalar
        def _(eng):
            chain = [0]

            def link(ins):
                chain[0] += 1
                ins.then_inc(act_chain, 1)
                eng.wait_ge(act_chain, chain[0])

            def layer_norm(f):
                for k in range(2):
                    i = slice(k * HALF, (k + 1) * HALF)
                    eng.wait_ge(ln_centred, 2 * f + k + 1)
                    for c in range(k * HALF, (k + 1) * HALF):
                        last = eng.activation(junk[:, c], hn[:, c], ACT.Square, accum_out=st[:, 2, c:c + 1])
                    link(last)
                    link(eng.activation(st[:, 3, i], st[:, 2, i], ACT.Ln, bias=eps[:, 1:2], scale=1.0 / HID))
                    eng.activation(st[:, 4, i], st[:, 3, i], ACT.Exp, scale=-0.5).then_inc(ln_rstd, 1)
                for i in range(2):
                    eng.wait_ge(ln_tr, 4 * f + 2 * i + 1)
                    eng.activation(*move_hT(f, 0, i), ACT.Copy).then_inc(hT_act, 1)

            def feed_forward(j):
                eng.wait_ge(f_sub, j + 1)
                eng.activation(gt[:, :, :], lg[:, :, :], ACT.Exp).then_inc(f_exp, 1)
                for i in range(2):
                    eng.wait_ge(f_hwT, 2 * j + i + 1)
                    eng.activation(hwT[:, i * HALF:(i + 1) * HALF, :].rearrange("p c t -> p (c t)"),
                                   bank[6 + i][0:NROW, :], ACT.Copy).then_inc(f_hwTs, 1)

            eng.preload_act_table_set(LN_EXP)
            eng.wait_ge(ident_ready, 1)
            eng.wait_ge(in_small, 16 * N_SMALL)
            link(eng.activation(negA[:, :], negA[:, :], ACT.Exp))
            eng.activation(negA[:, :], negA[:, :], ACT.Copy, scale=-1.0).then_inc(nega_ready, 1)
            layer_norm(0)
            feed_forward(0)
            layer_norm(1)
            for b in range(B):
                eng.wait_ge(low_done, b + 1)
                eng.activation(faT[:, b * S:(b + 1) * S], bank[4 + b][:, :], ACT.Copy).then_inc(low_copied, 1)
            for b in range(B):
                eng.wait_ge(low_done, B + b + 1)
                eng.activation(gaT[:, :, b, :], bank[6 + b][:, :].rearrange("p (c i) -> p c i", i=C),
                               ACT.Copy).then_inc(low_copied, 1)
            eng.wait_ge(beta_done, 1)
            eng.activation(btok[:, :, :].rearrange("p c h -> p (c h)"), bank[2][:, 0:NCH * H], ACT.Exp,
                           scale=-1.0).then_inc(beta_exp, 1)
            for i in range(2):
                eng.wait_ge(beta_turned, i + 1)
                eng.activation(beta16[:, i * HALF * P:(i + 1) * HALF * P], bank[i][0:H, :], ACT.Copy).then_inc(beta_copied, 1)
            eng.drain().then_inc(act_free, 1)

            def item(g, hh, b):
                j = hh * B + b
                i = g * ITEMS + j
                eng.wait_ge(q_done, i + 1)
                if j:
                    eng.wait_ge(n_done, 2 * i)
                eng.activation(sq[:, 0], bank[0][:, :], ACT.Square).then_inc(sq_ready, 1)
                eng.wait_ge(k_done, i + 1)
                eng.activation(sq[:, 1], bank[1][:, :], ACT.Square).then_inc(sq_ready, 1)
                for t in range(2):
                    eng.wait_ge(n_done, 2 * i + t + 1)
                    if j:
                        eng.wait_ge(normed, 2 * i - 1 + t)
                    eng.activation(rr[:, t], bank[5 + t][:, :], ACT.Ln, bias=eps[:, 0:1]).then_inc(n_ln, 1)
                    eng.wait_ge(n_ln, 2 * i + t + 1)
                    eng.activation(rr[:, t], rr[:, t], ACT.Exp, scale=-0.5).then_inc(r_ready, 1)
                if j:
                    decays(i - 1, *divmod(j - 1, B))
                eng.wait_ge(v_done, i + 1)
                if j:
                    eng.wait_ge(v_chain, (TAPS - 1) * i)
                for tap in range(TAPS):
                    o = vtap[tap] if tap < TAPS - 1 else qkv[:, 2, hh, b, :]
                    last = eng.activation(o, bank[2][:, :], ACT.Copy, scale=gchan[:, 2 * TAPS + tap, hh:hh + 1])
                last.then_inc(v_taps, 1)
                eng.wait_ge(z_ready, i + 1)
                eng.activation(zc, zc, ACT.Exp).then_inc(z_exp, 1)
                eng.wait_ge(z_exp, i + 1)
                if j:
                    eng.wait_ge(dec_ready, i)
                eng.activation(sp, zc, ACT.Ln, bias=1.0).then_inc(z_ln, 1)

            def decays(i, hh, b):
                eng.wait_ge(sp_ready, i + 1)
                eng.activation(dec[:, hh, b], sp, ACT.Exp, scale=gnegA[:, hh:hh + 1]).then_inc(dec_ready, 1)

            def head(n, c, p):
                eng.activation(gbi(ks[:, p]), chunk(qkv[:, 1], c), ACT.Silu).then_inc(ks_ready, 1)
                eng.activation(gbi(qs[:, :]), chunk(qkv[:, 0], c), ACT.Silu).then_inc(qs_ready, 1)
                eng.activation(gbi(es), chunk(dec, c), ACT.Copy).then_inc(es_ready, 1)

            def slot(g, n, c, p, step=True, scan=True, following=True):
                m, q = n - 1, 1 - p

                def inverse(l):
                    h = LEVELS[l]
                    if l < NL - 1:
                        eng.wait_ge(tm_done, (NL - 2) * n + l)
                        eng.activation(half(tmat, h, 0), blocks(bank[3][:, 0:HU], h), ACT.Copy).then_inc(tm_ready, 1)
                    eng.wait_ge(tt_done, (NL - 1) * n + l)
                    eng.activation(half(tt[:, p], h, 1), blocks(bank[2][:, HU:UN], h), ACT.Copy).then_inc(tt_ready, 1)

                def gates(*chunks):
                    if not scan:
                        for gc in chunks:
                            eng.wait_ge(gate_done, NCH * g + gc + 1)
                            eng.activation(gate[:, gc], bank[GATE_BANKS[gc % 2]][:, :], ACT.Tanh, scale=0.5).then_inc(gated, 1)

                if step:
                    eng.wait_ge(kq_ready, n + 1)
                    eng.activation(gbi(vs[:, :]), chunk(qkv[:, 2], c), ACT.Silu).then_inc(vs_ready, 1)
                if scan:
                    eng.wait_ge(u_done, n)
                    eng.activation(us, bank[4][:, :], ACT.Copy).then_inc(us_ready, 1)
                gates(0, 1)
                if step:
                    inverse(1)
                gates(2, 3)
                if scan:
                    eng.wait_ge(o_done, n)
                    eng.activation(osq, bank[5][:, :], ACT.Square).then_inc(osq_ready, 1)
                if step:
                    inverse(2)
                if following:
                    eng.wait_ge(vt_done, n + 1)
                    eng.wait_ge(updated, NL * n + 1)
                    head(n + 1, c + 1, q)
                gates(4)
                if step:
                    inverse(3)
                gates(5, 6)
                if scan:
                    eng.wait_ge(ot_done, n)
                    eng.activation(oT, bank[7][:, :], ACT.Copy).then_inc(ot_ready, 1)
                gates(7)
                if step:
                    inverse(4)
                    eng.wait_ge(kst_done, n + 1)
                    eng.activation(kst, bank[7][:, :], ACT.Copy).then_inc(kst_ready, 1)
                    inverse(5)

            with eng.Fori(0, NG) as g:
                n0 = g * NCH
                barrier(eng, act_free, g)
                eng.wait_ge(gprep, g + 1)
                for hh in range(G):
                    for b in range(B):
                        item(g, hh, b)
                decays(g * ITEMS + ITEMS - 1, G - 1, B - 1)
                eng.preload_act_table_set(SILU_TANH)

                eng.wait_ge(conved, 2 * ITEMS * g + 2 * ITEMS)
                eng.wait_ge(v_chain, (TAPS - 1) * ITEMS * g + (TAPS - 1) * ITEMS)
                eng.wait_ge(dec_ready, ITEMS * g + ITEMS)
                head(n0, 0, 0)
                run_slots(eng, slot, g)
                eng.preload_act_table_set(LN_EXP)
                eng.drain().then_inc(act_free, 1)
            layer_norm(2)
            feed_forward(1)

        @block.tensor
        def _(eng):
            def layer_norm(f):
                for i in range(2):
                    eng.wait_ge(ln_ready, 2 * f + i + 1)
                    for kt in range(KT):
                        for c in range(HALF):
                            last = eng.transpose(bank[2 * kt + i][:, c * P:(c + 1) * P],
                                                 hn[:, i * HALF + c, kt * P:(kt + 1) * P], ident[:, :])
                        last.then_inc(ln_tr, 1)
                eng.wait_ge(hT_act, 2 * f + 2)
                eng.wait_ge(hT_dve, 2 * f + 2)

            def feed_forward(j):
                if j == 0:
                    eng.wait_ge(in_ffn, 16 * N_FFN)
                for c in range(NCH):
                    o = bank[4 + c // HALF][:, (c % HALF) * P:]
                    for kt in range(KT):
                        eng.matmul(o[:, 0:RW + E], hT[:, kt, c * P:(c + 1) * P], w_a[:, kt, :],
                                   start=(kt == 0), stop=False)
                    last = eng.matmul(o[:, RW:RW + E], ones[0:1, :], brow[:, :], start=False, stop=True)
                    if c % HALF == HALF - 1:
                        last.then_inc(f_low, 1)
                for c in range(NCH):
                    for kt in range(KT):
                        eng.matmul(bank[c // 2][:, (c % 2) * HID:(c % 2 + 1) * HID], hT[:, kt, c * P:(c + 1) * P],
                                   w_base[:, kt, :], start=(kt == 0 and c % 2 == 0), stop=False, skip_group_check=True)
                eng.wait_ge(f_hw, j + 1)
                for c in range(NCH):
                    last = eng.transpose(bank[6 + c // HALF][0:NROW, (c % HALF) * P:(c % HALF + 1) * P],
                                         hw[:, c, :], ident[:, :])
                    if c % HALF == HALF - 1:
                        last.then_inc(f_hwT, 1)
                for c in range(NCH):
                    o = bank[c // 2][:, (c % 2) * HID:(c % 2 + 1) * HID]
                    if c % HALF == 0:
                        eng.wait_ge(f_hwTs, 2 * j + c // HALF + 1)
                    last = eng.matmul(o, hwT[:, c, :], w_b[:, :], start=False, stop=True, skip_group_check=True)
                    if c % 2:
                        last.then_inc(f_out, 1)

            eng.wait_ge(ident_ready, 1)
            eng.wait_ge(in_small, 16 * N_SMALL)
            nrow2 = TAPS * H + H + 1
            eng.transpose(bank[4][:, 0:P], rows1[:, :], ident[:, :])
            eng.transpose(bank[5][:, 0:nrow2], rows2[0:nrow2, :], ident[0:nrow2, 0:nrow2]).then_inc(rows_done, 1)
            layer_norm(0)
            eng.wait_ge(chan_ready, 1)
            feed_forward(0)
            layer_norm(1)
            eng.wait_ge(in_low, 16 * N_LOW)
            for w, o in ((wfa, 4), (wga, 6)):
                for b in range(B):
                    for kt in range(KT):
                        last = eng.matmul(bank[o + b][:, :], w[:, kt, :], hT[:, kt, b * S:(b + 1) * S],
                                          start=(kt == 0), stop=(kt == KT - 1))
                    last.then_inc(low_done, 1)
            for b in range(B):
                for c in range(NCH):
                    for kt in range(KT):
                        last = eng.matmul(bank[2][b * C:(b + 1) * C, c * H:(c + 1) * H],
                                          hT[:, kt, b * S + c * C:b * S + (c + 1) * C],
                                          wbeta[:, kt, :], start=(kt == 0), stop=(kt == KT - 1))
            last.then_inc(beta_done, 1)
            eng.wait_ge(low_copied, 2 * B)
            eng.wait_ge(beta_ready, 1)
            for c in range(NCH):
                last = eng.transpose(bank[c // HALF][0:H, (c % HALF) * P:(c % HALF + 1) * P], btok[:, c, :], ident[:, :])
                if c % HALF == HALF - 1:
                    last.then_inc(beta_turned, 1)
            eng.wait_ge(beta_copied, 2)
            eng.wait_ge(const_ready, 1)
            eng.drain().then_inc(pe_free, 1)

            def project(g, hh, b):
                j = hh * B + b
                i = g * ITEMS + j
                cols = slice(hh * D, (hh + 1) * D)
                toks = slice(b * S, (b + 1) * S)

                def columns(t, freed, value, done):
                    if j:
                        eng.wait_ge(freed, value)
                    for kt in range(KT):
                        last = eng.matmul(bank[t][:, :], gw[:, t, kt, cols], hT[:, kt, toks],
                                          start=(kt == 0), stop=(kt == KT - 1))
                    last.then_inc(done, 1)

                columns(0, normed, 2 * i - 1, q_done)
                columns(1, normed, 2 * i, k_done)
                for t in range(2):
                    eng.wait_ge(sq_ready, 2 * i + t + 1)
                    if j:
                        eng.wait_ge(n_ln, 2 * i - 1 + t)
                    eng.matmul(bank[5 + t][:, :], ones[:, :], sq[:, t], start=True, stop=True).then_inc(n_done, 1)
                columns(2, v_taps, i, v_done)
                if j:
                    eng.wait_ge(sp_ready, i)
                eng.matmul(bank[3][:, :], gfb[:, cols], faT[:, toks], start=True, stop=True).then_inc(f_done, 1)

            def level_products(n, p, l):
                h = LEVELS[l]
                if l == 0:
                    eng.wait_ge(kq_ready, n + 1)
                else:
                    eng.wait_ge(updated, NL * n + l)
                o = bank[l % 2][:, :].rearrange("p (a u t) -> p a u t", a=2, u=G)
                for u in range(G):
                    last = eng.matmul(o[:, :, u, :].rearrange("p a (n t) -> p a n t", t=h), unit(ks[:, p], u),
                                      half(kq[:, p, :, u * P:(u + 1) * P], h, 1), start=True, stop=True)
                last.then_inc(level_done, 1)

            def head_beta(c):
                for u in range(G):
                    last = eng.matmul(unit(bank[6], u), gsel[:, u:u + 1].broadcast_to((H, P)),
                                      beta16[:, ds(c * P, P)],
                                      start=True, stop=True)
                last.then_inc(b_done, 1)

            def head_diagonal(n, p):
                eng.wait_ge(qk_ready, n + 1)
                for u in range(G):
                    last = eng.matmul(bank[5][:, u:u + 1], unit(kq[:, p, 1], u), ones[:, 0:1], start=True, stop=True)
                last.then_inc(diag_done, 1)

            def slot(g, n, c, p, step=True, scan=True, following=True):
                m, q = n - 1, 1 - p

                def level(l):
                    level_products(n, p, l)

                def inverse_y(l):
                    h = LEVELS[l]
                    eng.wait_ge(n_ready, NL * n + l + 1)
                    if l == 1:
                        eng.wait_ge(f_ready, NL * n + 1)
                    elif l:
                        eng.wait_ge(tm_ready, (NL - 2) * n + l - 1)
                        eng.wait_ge(tt_ready, (NL - 1) * n + l - 1)
                    elif scan:
                        eng.wait_ge(tt_ready, (NL - 1) * n)
                    for u in range(G):
                        if l == 0:
                            last = eng.transpose(unit(bank[2], u), unit(nmat[:, 0], u), ident[:, :])
                        else:
                            last = eng.matmul(bank[2][:, u * C:(u + 1) * C].rearrange("p (n t) -> p n t", t=h),
                                              unit(nmat[:, l], u), half(unit(tmat, u), h, 0), start=True, stop=True)
                    last.then_inc(y_done, 1)

                def inverse_t(l):
                    h = LEVELS[l]
                    eng.wait_ge(f_ready, NL * n + l + 1)
                    if l == 1:
                        eng.wait_ge(tt0_ready, n + 1)
                    else:
                        eng.wait_ge(tt_ready, (NL - 1) * n + l - 1)
                    if l < NL - 1:
                        for u in range(G):
                            last = eng.matmul(bank[3][:, u * C:(u + 1) * C].rearrange("p (n t) -> p n t", t=h),
                                              unit(tt[:, p], u), half(unit(fmat[:, l - 1], u), h, 0), start=True, stop=True)
                        last.then_inc(tm_done, 1)
                    for u in range(G):
                        last = eng.matmul(bank[2][:, HU + u * C:HU + (u + 1) * C].rearrange("p (n t) -> p n t", t=h),
                                          unit(fmat[:, l - 1], u), half(unit(tt[:, p], u), h, 1), start=True, stop=True)
                    last.then_inc(tt_done, 1)

                def state_add(b):
                    rows = slice(b * C, (b + 1) * C)
                    for u in range(G):
                        last = eng.matmul(unit(bank[6], u), unit(kst, u)[rows, :], unit(us, u)[rows, :],
                                          start=True, stop=True)
                    last.then_inc(s_done, 1)

                def gates(*chunks):
                    if not scan:
                        for gc in chunks:
                            if gc >= 2:
                                eng.wait_ge(gated, NCH * g + gc - 1)
                            eng.matmul(bank[GATE_BANKS[gc % 2]][:, :], gaT[:, gc].rearrange("p b i -> p (b i)"), ggb[:, :],
                                       start=True, stop=True).then_inc(gate_done, 1)

                if scan:
                    eng.wait_ge(state_ready, B * m + g + 1)
                    for b in range(B):
                        for u in range(G):
                            last = eng.matmul(unit(bank[4], u)[b * C:(b + 1) * C, :],
                                              kq[:, q, 0, u * P + b * C:u * P + (b + 1) * C],
                                              unit(state[:, b], u), start=True, stop=True)
                    last.then_inc(r_done, 1)
                if step:
                    level(1)
                    inverse_y(0)
                gates(0, 1)
                if scan:
                    if step:
                        eng.wait_ge(diag_ready, n + 1)
                    for b in range(B):
                        for u in range(G):
                            eng.matmul(unit(bank[5], u)[b * C:(b + 1) * C, :],
                                       kq[:, q, 1, u * P + b * C:u * P + (b + 1) * C],
                                       unit(state[:, b], u), start=(u == 0), stop=False, skip_group_check=True)
                if step:
                    level(2)
                    inverse_y(1)
                if scan:
                    eng.wait_ge(rs_ready, n)
                    eng.wait_ge(tt_ready, (NL - 1) * n)
                    for u in range(G):
                        last = eng.matmul(unit(bank[4], u), unit(tt[:, q], u), unit(rs, u), start=True, stop=True)
                    last.then_inc(u_done, 1)
                gates(2)
                if step:
                    inverse_t(1)
                    level(3)
                gates(3)
                if scan:
                    eng.wait_ge(us_ready, n)
                    eng.wait_ge(aq_ready, NL * n)
                    for u in range(G):
                        last = eng.matmul(unit(bank[5], u), unit(aq[:, q], u), unit(us, u), start=False, stop=True,
                                          skip_group_check=True)
                    last.then_inc(o_done, 1)
                if step:
                    inverse_y(2)
                gates(4)
                if scan:
                    eng.wait_ge(kst_ready, n)
                    state_add(0)
                if step:
                    inverse_t(2)
                    level(4)
                    eng.wait_ge(vs_ready, n + 1)
                    for u in range(G):
                        last = eng.transpose(unit(bank[7], u), unit(vs, u), ident[:, :])
                    last.then_inc(vt_done, 1)
                    inverse_y(3)
                gates(5)
                if scan:
                    eng.wait_ge(state_ready, B * m + g + 2)
                    state_add(1)
                if step:
                    inverse_t(3)
                    level(5)
                gates(6)
                if step:
                    eng.wait_ge(vb_ready, n + 1)
                if scan:
                    eng.wait_ge(on_ready, n)
                    for u in range(G):
                        last = eng.transpose(unit(bank[7], u), unit(og, u), ident[:, :])
                    last.then_inc(ot_done, 1)
                if step:
                    inverse_y(4)
                gates(7)
                if following:
                    eng.wait_ge(state_ready, B * n + g + 1)
                    if not scan:
                        eng.wait_ge(gated, NCH * g + NCH)
                    head_beta(c + 1)
                if step:
                    inverse_t(4)
                    eng.wait_ge(updated, NL * n + NL)
                if scan:
                    eng.wait_ge(ot_ready, n)
                if step:
                    for u in range(G):
                        last = eng.transpose(unit(bank[7], u), unit(ks[:, p], u), ident[:, :])
                    last.then_inc(kst_done, 1)
                if following:
                    if scan:
                        eng.wait_ge(og_ready, n)
                    head_diagonal(n + 1, q)
                if step:
                    inverse_y(5)
                if scan:
                    for u in range(G):
                        last = eng.matmul(bank[4][:, 0:HID], unit(oT, u), gwo[:, u, :], start=(u == 0), stop=(u == G - 1))
                    last.then_inc(wo_done, 1)
                if step:
                    inverse_t(5)
                if following:
                    level_products(n + 1, q, 0)
                if step and scan:
                    eng.wait_ge(x_added, n)

            with eng.Fori(0, NG) as g:
                barrier(eng, pe_free, g)
                eng.wait_ge(in_group, 16 * N_GROUP * g + 16 * N_GROUP)
                eng.wait_ge(gprep, g + 1)
                for hh in range(G):
                    for b in range(B):
                        project(g, hh, b)
                last_item = ITEMS * g + ITEMS
                eng.wait_ge(n_ln, 2 * last_item)
                head_beta(0)
                head_diagonal(g * NCH, 0)
                eng.wait_ge(normed, 2 * last_item)
                eng.wait_ge(v_taps, last_item)
                eng.wait_ge(sp_ready, last_item)
                level_products(g * NCH, 0, 0)
                eng.wait_ge(wos_ready, g + 1)
                run_slots(eng, slot, g)
                eng.drain().then_inc(pe_free, 1)
            layer_norm(2)
            feed_forward(1)

        @block.vector
        def _(eng):
            chain = [0]

            def link(ins):
                chain[0] += 1
                ins.then_inc(dve_chain, 1)
                eng.wait_ge(dve_chain, chain[0])

            def layer_norm(f):
                tiles = [slice(i * HALF, (i + 1) * HALF) for i in range(2)]
                for i in tiles:
                    link(eng.tensor_reduce(st[:, 0, i], x[:, i, :], AX.X, ALU.add))
                    link(eng.tensor_scalar(st[:, 1, i], st[:, 0, i], 1.0 / HID, None, ALU.mult))
                    eng.tensor_tensor(hn[:, i], x[:, i, :], spread(st[:, 1, i], HID), ALU.subtract).then_inc(ln_centred, 1)
                for k, i in enumerate(tiles):
                    eng.wait_ge(ln_rstd, 2 * f + k + 1)
                    eng.tensor_tensor(hn[:, i], hn[:, i], spread(st[:, 4, i], HID), ALU.mult).then_inc(ln_ready, 1)
                for i in range(2):
                    eng.wait_ge(ln_tr, 4 * f + 2 * i + 2)
                    eng.tensor_copy(*move_hT(f, 1, i)).then_inc(hT_dve, 1)

            def feed_forward(j):
                low = [bank[4 + i][:, :].rearrange("p (c r) -> p c r", c=HALF) for i in range(2)]
                tiles = [slice(i * HALF, (i + 1) * HALF) for i in range(2)]
                for i in range(2):
                    eng.wait_ge(f_low, 2 * j + i + 1)
                    last = eng.tensor_copy(lg[:, tiles[i], :], low[i][:, :, RW:RW + E])
                link(last)
                link(eng.tensor_reduce(sm[:, 0], lg[:, :, :], AX.X, ALU.max))
                eng.tensor_tensor(lg[:, :, :], lg[:, :, :], spread(sm[:, 0], E), ALU.subtract).then_inc(f_sub, 1)
                eng.wait_ge(f_exp, j + 1)
                link(eng.tensor_reduce(sm[:, 1], gt[:, :, :], AX.X, ALU.add))
                link(eng.reciprocal(sm[:, 2], sm[:, 1]))
                link(eng.tensor_tensor(gt[:, :, :], gt[:, :, :], spread(sm[:, 2], E), ALU.mult))
                for e in range(E):
                    o = rk if e == 0 else beats
                    ge = gt[:, :, e:e + 1]
                    last = eng.tensor_tensor(o[:, :, 0:e + 1], ge.broadcast_to((P, NCH, e + 1)), gt[:, :, 0:e + 1], ALU.is_gt)
                    if e < E - 1:
                        last = eng.tensor_tensor(o[:, :, e + 1:E], ge.broadcast_to((P, NCH, E - 1 - e)),
                                                 gt[:, :, e + 1:E], ALU.is_ge)
                    link(last)
                    if e:
                        link(eng.tensor_tensor(rk[:, :, :], rk[:, :, :], beats[:, :, :], ALU.add))
                link(eng.scalar_tensor_tensor(out=gt[:, :, :], in0=rk[:, :, :], scalar=float(TOP), in1=gt[:, :, :],
                                              op0=ALU.is_lt, op1=ALU.mult))
                eng.memset(hw[:, :, RW:NROW], 1.0)
                for i in range(2):
                    eng.tensor_copy(hw[:, tiles[i], 0:R], low[i][:, :, 0:R])
                    last = eng.tensor_tensor(
                        hw[:, tiles[i], R:RW].rearrange("p c (e r) -> p c e r", e=E),
                        low[i][:, :, R:RW].rearrange("p c (e r) -> p c e r", e=E),
                        gt[:, tiles[i], :].rearrange("p c (e o) -> p c e o", o=1).broadcast_to((P, HALF, E, R)), ALU.mult)
                last.then_inc(f_hw, 1)
                for i in range(NCH // 2):
                    eng.wait_ge(f_out, NCH // 2 * j + i + 1)
                    v = x[:, 2 * i:2 * i + 2, :].rearrange("p c d -> p (c d)")
                    last = eng.scalar_tensor_tensor(out=v, in0=bank[i][:, :], scalar=0.5, in1=v, op0=ALU.mult, op1=ALU.add)
                last.then_inc(x_ready, 1)
                eng.wait_ge(x_ready, j + 1)

            eng.wait_ge(in_x, 16 * B)
            layer_norm(0)
            flat = chan[:, :, :].rearrange("p r h -> p (r h)")
            nrow2 = TAPS * H + H
            eng.wait_ge(rows_done, 1)
            eng.tensor_copy(flat[:, 0:P], bank[4][:, 0:P])
            eng.tensor_copy(flat[:, P:P + nrow2], bank[5][:, 0:nrow2])
            eng.tensor_copy(rmsc[:, :], bank[5][:, nrow2:nrow2 + 1]).then_inc(chan_ready, 1)
            feed_forward(0)
            layer_norm(1)
            eng.wait_ge(beta_exp, 1)
            link(eng.tensor_scalar(btok[:, :, :], btok[:, :, :], 1.0, None, ALU.add))
            eng.reciprocal(btok[:, :, :], btok[:, :, :]).then_inc(beta_ready, 1)
            eng.wait_ge(chan_ready, 1)
            eng.wait_ge(nega_ready, 1)
            eng.wait_ge(beta_ready, 1)
            eng.drain().then_inc(dve_free, 1)

            def item(g, hh, b):
                j = hh * B + b
                i = g * ITEMS + j
                chained = 2 * (TAPS - 1)
                bias = gchan[:, DT, hh:hh + 1]

                def conv(tap):
                    for t in range(2):
                        o = qkv[:, t, hh, b, :]
                        src = pad[:, t, tap:tap + S]
                        w = gchan[:, t * TAPS + tap, hh:hh + 1]
                        if tap == 0:
                            last = eng.tensor_scalar(o, src, w, None, ALU.mult)
                        else:
                            eng.wait_ge(conv_chain, chained * i + 2 * (tap - 1) + t + 1)
                            last = eng.scalar_tensor_tensor(out=o, in0=src, scalar=w, in1=o, op0=ALU.mult, op1=ALU.add)
                        last.then_inc(conv_chain if tap < TAPS - 1 else conved, 1)

                for t in range(2):
                    if j:
                        eng.wait_ge(conved, 2 * i - 1 + t)
                    eng.wait_ge(r_ready, 2 * i + t + 1)
                    eng.tensor_tensor(pad[:, t, TAPS - 1:], bank[t][:, :], rr[:, t], ALU.mult).then_inc(normed, 1)
                eng.wait_ge(normed, 2 * i + 2)
                conv(0)
                eng.wait_ge(f_done, i + 1)
                if j:
                    eng.wait_ge(z_ln, i)
                eng.tensor_scalar(zc, bank[3][:, :], bias, SOFT_MAX, ALU.add, ALU.min).then_inc(z_ready, 1)
                conv(1)
                conv(2)
                eng.wait_ge(z_ln, i + 1)
                eng.scalar_tensor_tensor(out=sp, in0=bank[3][:, :], scalar=bias, in1=sp,
                                         op0=ALU.add, op1=ALU.max).then_inc(sp_ready, 1)
                conv(3)

            def decays(n, p, l):
                h = LEVELS[l]
                lower, upper = (tots[l].rearrange("p (n t) -> p n t", t=2)[:, :, i] for i in range(2))
                nb = HU // h
                if l:
                    eng.wait_ge(aq_ready, NL * n + l)
                else:
                    eng.wait_ge(diag_ready, n + 1)
                eng.wait_ge(level_done, NL * n + l + 1)
                eng.tensor_tensor(half(kq[:, p], h, 1), half(kq[:, p], h, 1),
                                  lower.rearrange("p (a n o) -> p a n o", a=1, o=1).broadcast_to((P, 2, nb, h)), ALU.mult)
                eng.tensor_tensor(half(ks[:, p], h, 0), half(ks[:, p], h, 0), spread(upper, h), ALU.mult)
                eng.tensor_tensor(tots[l + 1] if l < NL - 1 else gamma[:, p], lower, upper, ALU.mult).then_inc(updated, 1)

            def keep_pairs(n, p, l):
                h = LEVELS[l]
                mask = blocks(masks[:, l], h)
                eng.copy_predicated(half(nmat[:, l], h, 1), mask, blocks(bank[l % 2][:, 0:HU], h)).then_inc(n_ready, 1)
                eng.copy_predicated(half(aq[:, p], h, 1), mask, blocks(bank[l % 2][:, HU:UN], h)).then_inc(aq_ready, 1)

            def head(n, p):
                eng.wait_ge(b_done, n + 1)
                eng.wait_ge(ks_ready, n + 1)
                eng.tensor_tensor(kq[:, p, 0], ks[:, p], bank[6][:, :], ALU.mult).then_inc(kb_ready, 1)
                eng.wait_ge(diag_done, n + 1)
                eng.wait_ge(es_ready, n + 1)
                eng.tensor_tensor(kq[:, p, 1], qs[:, :], es, ALU.mult)
                eng.wait_ge(kb_ready, n + 1)
                eng.tensor_tensor(kq[:, p, 0], kq[:, p, 0], es, ALU.mult).then_inc(kq_ready, 1)
                eng.tensor_tensor(gd(aq[:, p]), ident4, spread(bank[5][:, 0:G], P), ALU.mult).then_inc(diag_ready, 1)

            def slot(g, n, c, p, step=True, scan=True, following=True):
                m, q = n - 1, 1 - p

                def level(l):
                    decays(n, p, l)

                def keep(l):
                    keep_pairs(n, p, l)

                def inverse(l):
                    h = LEVELS[l]
                    eng.wait_ge(y_done, NL * n + l + 1)
                    if l == 0:
                        eng.tensor_tensor(gd(tmat), ident4, gd(bank[2][:, :]), ALU.subtract).then_inc(f_ready, 1)
                    else:
                        lower = [v.rearrange("p u (n t) -> p u n t", t=2 * h)[:, :, :, 0:h] for v in (gd(fmat[:, l - 1]), ident4)]
                        eng.tensor_tensor(lower[0], lower[1],
                                          bank[2][:, 0:HU].rearrange("p (u n t) -> p u n t", u=G, t=h),
                                          ALU.subtract).then_inc(f_ready, 1)

                def add_state(b):
                    eng.wait_ge(sdec_ready, B * m + b + 1)
                    eng.wait_ge(s_done, B * m + b + 1)
                    eng.tensor_tensor(state[:, b], sdec[:, b], bank[6][:, :], ALU.add).then_inc(state_ready, 1)

                if scan:
                    eng.wait_ge(r_done, n)
                    eng.wait_ge(vb_ready, n)
                    eng.tensor_tensor(rs, vb, bank[4][:, :], ALU.subtract).then_inc(rs_ready, 1)
                if step:
                    level(1)
                    inverse(0)
                    keep(1)
                    level(2)
                    inverse(1)
                    keep(2)
                if step:
                    level(3)
                    inverse(2)
                    keep(3)
                if scan:
                    add_state(0)
                    eng.wait_ge(osq_ready, n)
                    eng.tensor_reduce(ssq[:, 0], gd(osq), AX.X, ALU.add).then_inc(ssq_ready, 1)
                    eng.scalar_tensor_tensor(out=og, in0=gate[:, ds(c - 1, 1), :].rearrange("p a d -> p (a d)"),
                                             scalar=1.0, in1=bank[5][:, :], op0=ALU.add, op1=ALU.mult).then_inc(og_ready, 1)
                if step:
                    level(4)
                    eng.wait_ge(vt_done, n + 1)
                    eng.tensor_tensor(gd(vb), gd(bank[7][:, :]),
                                      spread(btok[:, ds(c, 1), ds(g * G, G)].rearrange("p a h -> p (a h)"), D),
                                      ALU.mult).then_inc(vb_ready, 1)
                    inverse(3)
                    keep(4)
                if scan:
                    add_state(1)
                if step:
                    level(5)
                    inverse(4)
                    keep(5)
                if following:
                    head(n + 1, q)
                if step:
                    inverse(5)
                if scan:
                    eng.wait_ge(wo_done, n)
                    v = x[:, ds(c - 1, 1), :].rearrange("p a d -> p (a d)")
                    eng.tensor_tensor(v, v, bank[4][:, 0:HID], ALU.add).then_inc(x_added, 1)
                if following:
                    decays(n + 1, q, 0)
                    keep_pairs(n + 1, q, 0)

            with eng.Fori(0, NG) as g:
                barrier(eng, dve_free, g)
                heads = ds(g * G, G)
                eng.memset(pad[:, :, 0:TAPS - 1], 0.0)
                eng.tensor_copy(gchan[:, :, :], chan[:, :, heads])
                eng.tensor_copy(gnegA[:, :], negA[:, heads])
                eng.tensor_copy(gsel[:, :], ident[0:H, heads]).then_inc(gprep, 1)
                eng.memset(state[:, :, :], 0.0).then_inc(state_ready, 1)
                eng.wait_ge(gprep, g + 1)
                for hh in range(G):
                    for b in range(B):
                        item(g, hh, b)
                eng.wait_ge(in_wo, 16 * g + 16)
                eng.tensor_scalar(gwo[:, :, :], gwo[:, :, :], rmsc[:, :], 0.5 * float(D) ** 0.5, ALU.mult, ALU.mult).then_inc(wos_ready, 1)
                head(g * NCH, 0)
                decays(g * NCH, 0, 0)
                keep_pairs(g * NCH, 0, 0)
                run_slots(eng, slot, g)
                eng.drain().then_inc(dve_free, 1)
            layer_norm(2)
            feed_forward(1)


_PRE = {"L0_attn_hidden_states": "x"}
_INS = ["L0_attn_hidden_states", "L0_attn_Wq", "L0_attn_Wk", "L0_attn_Wv", "L0_attn_conv_q", "L0_attn_conv_k",
        "L0_attn_conv_v", "L0_attn_Wb", "L0_attn_Wfa", "L0_attn_Wfb", "L0_attn_Wga", "L0_attn_Wgb", "L0_attn_A_log",
        "L0_attn_dt_bias", "L0_attn_rms_scale", "L0_attn_Wo", "L0_ffn_W_base", "L0_ffn_b_base", "L0_ffn_A_s",
        "L0_ffn_B_s", "L0_ffn_A_r", "L0_ffn_B_r", "L0_ffn_W_router", "L0_ffn_b_router"]


def kernel(**inputs):
    import numpy as _np
    import concourse.bacc as _bacc
    from concourse import mybir as _mybir
    from concourse.bass_utils import run_bass_kernel_spmd as _run

    nc = _bacc.Bacc("TRN2", target_bir_lowering=False, num_devices=1)
    arrays, aps = {}, {}
    for name in _INS:
        v = _np.ascontiguousarray(inputs[name])
        arrays[f"in_{name}"] = v
        short = _PRE.get(name) or name.split("_", 2)[2]
        aps[short] = nc.dram_tensor(f"in_{name}", v.shape, _mybir.dt.from_np(v.dtype), kind="ExternalInput").ap()
    out = nc.dram_tensor("out", (B, S, HID), F32, kind="ExternalOutput").ap()
    build(nc, aps, out)
    r = _run(nc, [arrays], core_ids=[0])
    return r.results[0]["out"]
```
